# Optimizing a Trainium2 kernel written in Bass

```python
import numpy as np
import jax
import jax.numpy as jnp

def _softmax(x, axis=-1):
    return jax.nn.softmax(x, axis=axis)

def _gelu(x):
    return jax.nn.gelu(x, approximate=True)

def _silu(x):
    return jax.nn.silu(x)

def _sigmoid(x):
    return jax.nn.sigmoid(x)

def _layernorm(x, axis=-1, eps=1e-05):
    m = jnp.mean(x, axis=axis, keepdims=True)
    v = jnp.var(x, axis=axis, keepdims=True)
    return (x - m) / jnp.sqrt(v + eps)

def _scatter_add(tgt, idx, src, axis=0):
    return tgt.at[idx].add(src)

def _segment_sum(src, seg, n):
    return jax.ops.segment_sum(src, seg, n)
kernel_name = 'mk_hybrid_d1_jaxref_r8_7cfbf0'

def setup_inputs(seed: int=0):
    np.random.seed(seed)
    _w = jnp.asarray

    def _L0_attn_a_setup():
        import jax, jax.numpy as jnp
        import numpy as np
        B, L, D = (2, 256, 128)
        H, HD = (16, 64)
        LD = 32
        key = jax.random.key(seed)
        ks = jax.random.split(key, 6)
        s = lambda fan_in: 1.0 / np.sqrt(fan_in)
        x_bld = jax.random.normal(ks[0], (B, L, D), dtype=jnp.float32)
        Wq = jax.random.normal(ks[1], (D, H, HD), dtype=jnp.float32) * s(D)
        Wkv_down = jax.random.normal(ks[2], (D, LD), dtype=jnp.float32) * s(D)
        Wk_up = jax.random.normal(ks[3], (LD, H, HD), dtype=jnp.float32) * s(LD)
        Wv_up = jax.random.normal(ks[4], (LD, H, HD), dtype=jnp.float32) * s(LD)
        Wout = jax.random.normal(ks[5], (H, HD, D), dtype=jnp.float32) * s(H * HD)
        return {'x_bld': x_bld, 'Wq': Wq, 'Wkv_down': Wkv_down, 'Wk_up': Wk_up, 'Wv_up': Wv_up, 'Wout': Wout}
    _L0_attn_a_in = _L0_attn_a_setup()

    def _L0_attn_b_setup():
        import jax, jax.numpy as jnp
        import numpy as np
        D_MODEL = 128
        D_STATE = 128
        D_CONV = 4
        EXPAND = 2
        NHEADS = 32
        NGROUPS = 1
        D_INNER = EXPAND * D_MODEL
        HEADDIM = D_INNER // NHEADS
        CHUNK = 32
        BATCH, SEQLEN = (2, 256)
        D_IN_PROJ = 2 * D_INNER + 2 * NGROUPS * D_STATE + NHEADS
        CONV_DIM = D_INNER + 2 * NGROUPS * D_STATE
        LN_EPS = 1e-05

        def _segsum(x):
            T = x.shape[-1]
            cs = jnp.cumsum(x, axis=-1)
            diff = cs[..., :, None] - cs[..., None, :]
            mask = jnp.tril(jnp.ones((T, T), bool))
            return jnp.where(mask, diff, -jnp.inf)

        def _ssd_chunked(X, A, B, C, chunk):
            b, l, h, p = X.shape
            c = l // chunk
            X = X.reshape(b, c, chunk, h, p)
            B = B.reshape(b, c, chunk, h, -1)
            C = C.reshape(b, c, chunk, h, -1)
            A = A.reshape(b, c, chunk, h).transpose(0, 3, 1, 2)
            A_cs = jnp.cumsum(A, axis=-1)
            L = jnp.exp(_segsum(A))
            Y_diag = jnp.einsum('bclhn,bcshn,bhcls,bcshp->bclhp', C, B, L, X)
            decay_states = jnp.exp(A_cs[..., -1:] - A_cs)
            states = jnp.einsum('bclhn,bhcl,bclhp->bchpn', B, decay_states, X)
            states = jnp.concatenate([jnp.zeros_like(states[:, :1]), states], axis=1)
            decay_chunk = jnp.exp(_segsum(jnp.pad(A_cs[..., -1], ((0, 0), (0, 0), (1, 0)))))
            new_states = jnp.einsum('bhzc,bchpn->bzhpn', decay_chunk, states)
            states = new_states[:, :-1]
            Y_off = jnp.einsum('bclhn,bchpn,bhcl->bclhp', C, states, jnp.exp(A_cs))
            return (Y_diag + Y_off).reshape(b, l, h, p)
        key = jax.random.key(seed)
        ks = jax.random.split(key, 8)
        dt = jnp.exp(jax.random.uniform(ks[4], (NHEADS,)) * (np.log(0.1) - np.log(0.001)) + np.log(0.001))
        dt = jnp.clip(dt, 0.0001, None)
        inv_dt = dt + jnp.log(-jnp.expm1(-dt))
        A = jax.random.uniform(ks[5], (NHEADS,), minval=1.0, maxval=16.0)
        return {'u': jax.random.normal(ks[0], (BATCH, SEQLEN, D_MODEL), jnp.float32), 'in_proj_w': jax.random.normal(ks[1], (D_IN_PROJ, D_MODEL), jnp.float32) * D_MODEL ** (-0.5), 'conv_w': jax.random.normal(ks[2], (CONV_DIM, D_CONV), jnp.float32) * D_CONV ** (-0.5), 'conv_b': jnp.zeros((CONV_DIM,), jnp.float32), 'dt_bias': inv_dt.astype(jnp.float32), 'A_log': jnp.log(A).astype(jnp.float32), 'ln_w': jnp.ones((D_INNER,), jnp.float32), 'out_proj_w': jax.random.normal(ks[3], (D_MODEL, D_INNER), jnp.float32) * D_INNER ** (-0.5)}
    _L0_attn_b_in = _L0_attn_b_setup()

    def _L0_ffn_setup():
        import jax, jax.numpy as jnp
        import numpy as np
        TOP_K = 2
        EPS = 1e-20
        key = jax.random.key(seed)
        ks = jax.random.split(key, 8)
        B, S, H, E, D = (4, 256, 128, 8, 256)
        s = 0.02
        return {'x': jax.random.normal(ks[0], (B, S, H), dtype=jnp.float32), 'Wr': jax.random.normal(ks[1], (H, E), dtype=jnp.float32) * s, 'Wg': jax.random.normal(ks[2], (E, H, D), dtype=jnp.float32) * s, 'Wu': jax.random.normal(ks[3], (E, H, D), dtype=jnp.float32) * s, 'Wd': jax.random.normal(ks[4], (E, D, H), dtype=jnp.float32) * s, 'Sg': jax.random.normal(ks[5], (H, D), dtype=jnp.float32) * s, 'Su': jax.random.normal(ks[6], (H, D), dtype=jnp.float32) * s, 'Sd': jax.random.normal(ks[7], (D, H), dtype=jnp.float32) * s}
    _L0_ffn_in = _L0_ffn_setup()
    _d = {'L0_attn_a_x_bld': _L0_attn_a_in['x_bld'], 'L0_attn_a_Wq': _L0_attn_a_in['Wq'], 'L0_attn_a_Wkv_down': _L0_attn_a_in['Wkv_down'], 'L0_attn_a_Wk_up': _L0_attn_a_in['Wk_up'], 'L0_attn_a_Wv_up': _L0_attn_a_in['Wv_up'], 'L0_attn_a_Wout': _L0_attn_a_in['Wout'], 'L0_attn_b_in_proj_w': _L0_attn_b_in['in_proj_w'], 'L0_attn_b_conv_w': _L0_attn_b_in['conv_w'], 'L0_attn_b_conv_b': _L0_attn_b_in['conv_b'], 'L0_attn_b_dt_bias': _L0_attn_b_in['dt_bias'], 'L0_attn_b_A_log': _L0_attn_b_in['A_log'], 'L0_attn_b_ln_w': _L0_attn_b_in['ln_w'], 'L0_attn_b_out_proj_w': _L0_attn_b_in['out_proj_w'], 'L0_ffn_Wr': _L0_ffn_in['Wr'], 'L0_ffn_Wg': _L0_ffn_in['Wg'], 'L0_ffn_Wu': _L0_ffn_in['Wu'], 'L0_ffn_Wd': _L0_ffn_in['Wd'], 'L0_ffn_Sg': _L0_ffn_in['Sg'], 'L0_ffn_Su': _L0_ffn_in['Su'], 'L0_ffn_Sd': _L0_ffn_in['Sd']}
    _x0 = _d['L0_attn_a_x_bld']
    _d['L0_attn_a_x_bld'] = jax.random.normal(jax.random.fold_in(jax.random.key(seed), 1), (16, 512, 128), dtype=_x0.dtype)
    del _x0
    return _d

def reference(L0_attn_a_x_bld, L0_attn_a_Wq, L0_attn_a_Wkv_down, L0_attn_a_Wk_up, L0_attn_a_Wv_up, L0_attn_a_Wout, L0_attn_b_in_proj_w, L0_attn_b_conv_w, L0_attn_b_conv_b, L0_attn_b_dt_bias, L0_attn_b_A_log, L0_attn_b_ln_w, L0_attn_b_out_proj_w, L0_ffn_Wr, L0_ffn_Wg, L0_ffn_Wu, L0_ffn_Wd, L0_ffn_Sg, L0_ffn_Su, L0_ffn_Sd):

    def _L0_attn_a_ref(x_bld, Wq, Wkv_down, Wk_up, Wv_up, Wout):
        import jax, jax.numpy as jnp
        import numpy as np
        B, L, D = (2, 256, 128)
        H, HD = (16, 64)
        LD = 32
        q_blhd = jnp.einsum('bld,dhk->blhk', x_bld, Wq)
        latent_bll = jnp.einsum('bld,dc->blc', x_bld, Wkv_down)
        k_blhd = jnp.einsum('blc,chk->blhk', latent_bll, Wk_up)
        v_blhd = jnp.einsum('blc,chk->blhk', latent_bll, Wv_up)
        attn = jnp.einsum('bqhd,bkhd->bhqk', q_blhd, k_blhd) / jnp.sqrt(jnp.asarray(HD, dtype=x_bld.dtype))
        l = x_bld.shape[1]
        mask = (jnp.arange(l)[None, :] <= jnp.arange(l)[:, None])[None, None]
        neg_inf = jnp.finfo(attn.dtype).min
        attn = jax.nn.softmax(jnp.where(mask, attn, neg_inf), axis=-1)
        y_blhd = jnp.einsum('bhqk,bkhd->bqhd', attn, v_blhd)
        return jnp.einsum('bqhd,hdo->bqo', y_blhd, Wout)

    def _L0_attn_b_ref(u, in_proj_w, conv_w, conv_b, dt_bias, A_log, ln_w, out_proj_w):
        import jax, jax.numpy as jnp
        import numpy as np
        D_MODEL = 128
        D_STATE = 128
        D_CONV = 4
        EXPAND = 2
        NHEADS = 32
        NGROUPS = 1
        D_INNER = EXPAND * D_MODEL
        HEADDIM = D_INNER // NHEADS
        CHUNK = 32
        BATCH, SEQLEN = (2, 256)
        D_IN_PROJ = 2 * D_INNER + 2 * NGROUPS * D_STATE + NHEADS
        CONV_DIM = D_INNER + 2 * NGROUPS * D_STATE
        LN_EPS = 1e-05

        def _segsum(x):
            T = x.shape[-1]
            cs = jnp.cumsum(x, axis=-1)
            diff = cs[..., :, None] - cs[..., None, :]
            mask = jnp.tril(jnp.ones((T, T), bool))
            return jnp.where(mask, diff, -jnp.inf)

        def _ssd_chunked(X, A, B, C, chunk):
            b, l, h, p = X.shape
            c = l // chunk
            X = X.reshape(b, c, chunk, h, p)
            B = B.reshape(b, c, chunk, h, -1)
            C = C.reshape(b, c, chunk, h, -1)
            A = A.reshape(b, c, chunk, h).transpose(0, 3, 1, 2)
            A_cs = jnp.cumsum(A, axis=-1)
            L = jnp.exp(_segsum(A))
            Y_diag = jnp.einsum('bclhn,bcshn,bhcls,bcshp->bclhp', C, B, L, X)
            decay_states = jnp.exp(A_cs[..., -1:] - A_cs)
            states = jnp.einsum('bclhn,bhcl,bclhp->bchpn', B, decay_states, X)
            states = jnp.concatenate([jnp.zeros_like(states[:, :1]), states], axis=1)
            decay_chunk = jnp.exp(_segsum(jnp.pad(A_cs[..., -1], ((0, 0), (0, 0), (1, 0)))))
            new_states = jnp.einsum('bhzc,bchpn->bzhpn', decay_chunk, states)
            states = new_states[:, :-1]
            Y_off = jnp.einsum('bclhn,bchpn,bhcl->bclhp', C, states, jnp.exp(A_cs))
            return (Y_diag + Y_off).reshape(b, l, h, p)
        b, l, _ = u.shape
        zxbcdt = u @ in_proj_w.T
        z = zxbcdt[..., :D_INNER]
        xBC = zxbcdt[..., D_INNER:D_INNER + CONV_DIM]
        dt = jax.nn.softplus(zxbcdt[..., -NHEADS:] + dt_bias)
        A = -jnp.exp(A_log)
        xp = jnp.pad(xBC, ((0, 0), (D_CONV - 1, 0), (0, 0)))
        acc = conv_b
        for k in range(D_CONV):
            acc = acc + xp[:, k:k + l, :] * conv_w[:, k]
        xBC = jax.nn.silu(acc)
        x = xBC[..., :D_INNER].reshape(b, l, NHEADS, HEADDIM)
        Bm = xBC[..., D_INNER:D_INNER + NGROUPS * D_STATE].reshape(b, l, NGROUPS, D_STATE)
        Cm = xBC[..., D_INNER + NGROUPS * D_STATE:].reshape(b, l, NGROUPS, D_STATE)
        rep = NHEADS // NGROUPS
        Bh = jnp.repeat(Bm, rep, axis=2)
        Ch = jnp.repeat(Cm, rep, axis=2)
        y = _ssd_chunked(x * dt[..., None], A * dt, Bh, Ch, CHUNK)
        y = y.reshape(b, l, D_INNER)
        mu = y.mean(-1, keepdims=True)
        var = y.var(-1, keepdims=True)
        y = (y - mu) / jnp.sqrt(var + LN_EPS) * ln_w
        y = y * jax.nn.silu(z)
        return y @ out_proj_w.T

    def _L0_ffn_ref(x, Wr, Wg, Wu, Wd, Sg, Su, Sd):
        import jax, jax.numpy as jnp
        import numpy as np
        TOP_K = 2
        EPS = 1e-20
        B, S, H = x.shape
        T = B * S
        xt = x.reshape(T, H)
        scores = jax.nn.softmax(xt @ Wr, axis=-1)
        topk_w, topk_idx = jax.lax.top_k(scores, TOP_K)
        topk_w = topk_w / (topk_w.sum(axis=-1, keepdims=True) + EPS)
        g = jax.nn.silu(jnp.einsum('th,ehd->etd', xt, Wg))
        u = jnp.einsum('th,ehd->etd', xt, Wu)
        out_all = jnp.einsum('etd,edh->eth', g * u, Wd)
        tok = jnp.arange(T)[:, None]
        gathered = out_all[topk_idx, tok, :]
        out = jnp.sum(gathered * topk_w[..., None], axis=1).reshape(B, S, H)
        shared = jax.nn.silu(x @ Sg) * (x @ Su) @ Sd
        return out + shared
    x = L0_attn_a_x_bld
    x = x + _L0_attn_a_ref(_layernorm(x, axis=-1), L0_attn_a_Wq, L0_attn_a_Wkv_down, L0_attn_a_Wk_up, L0_attn_a_Wv_up, L0_attn_a_Wout)
    x = x + _L0_ffn_ref(_layernorm(x, axis=-1), L0_ffn_Wr, L0_ffn_Wg, L0_ffn_Wu, L0_ffn_Wd, L0_ffn_Sg, L0_ffn_Su, L0_ffn_Sd)
    x = x + _L0_attn_b_ref(_layernorm(x, axis=-1), L0_attn_b_in_proj_w, L0_attn_b_conv_w, L0_attn_b_conv_b, L0_attn_b_dt_bias, L0_attn_b_A_log, L0_attn_b_ln_w, L0_attn_b_out_proj_w)
    x = x + _L0_ffn_ref(_layernorm(x, axis=-1), L0_ffn_Wr, L0_ffn_Wg, L0_ffn_Wu, L0_ffn_Wd, L0_ffn_Sg, L0_ffn_Su, L0_ffn_Sd)
    return x

_drawn_inputs = setup_inputs


def setup_inputs(seed=0):
    import zlib

    import numpy as np

    out = dict(_drawn_inputs(seed))
    spreads = {'L0_attn_b_conv_b': (0.0, 0.1), 'L0_attn_b_ln_w': (1.0, 0.2)}
    factors = {'L0_ffn_Wr': 6.476,
     'L0_ffn_Wg': 5.608,
     'L0_ffn_Wu': 5.604,
     'L0_ffn_Wd': 5.582,
     'L0_ffn_Sg': 3.845,
     'L0_ffn_Su': 3.775,
     'L0_ffn_Sd': 3.8}
    for name, (base, spread) in spreads.items():
        noise = np.random.default_rng([zlib.crc32(name.encode()), seed]).standard_normal(out[name].shape)
        drawn = base * np.exp(spread * noise) if base else spread * noise
        out[name] = jnp.asarray(drawn.astype(out[name].dtype))
    for name, factor in factors.items():
        out[name] = (out[name] * factor).astype(out[name].dtype)
    return out
```

```python
from contextlib import ExitStack

import concourse.bass as bass
from concourse import mybir

F32 = mybir.dt.float32
F32R = mybir.dt.float32r
ALU = mybir.AluOpType
ACT = mybir.ActivationFunctionType
AX = mybir.AxisListType

P = 128
SEQS = 16
L = 512
QT = L // P
PAIRS = SEQS // 2
D = 128
LN_EPS = 1e-5
H, HD, LD = 16, 64, 32
HG = P // LD
G = H // HG
UNITS = 3
UPS = UNITS * H
MASKED = -1.0e30
E, F, TOPK = 8, 256, 2
FC = F // P
XP = E + 1
MU = XP * FC
ROUTE_EPS = 1e-20

DI, NS, NH, HP = 256, 128, 32, 8
TAPS, CH = 4, 32
CT = P // CH
NC = L // CH
XB = (DI + 2 * NS) // P
SG = NH // CT
ATANH = [1.0 / n for n in range(17, 1, -2)]

UNIT_TILES = [[(3, 0)], [(2, 0), (0, 384)], [(1, 0)]]
UNIT_COLS = [512, 512, 256]
UNIT_AT = [0, 512, 1024]
HEAD_COLS = 1280


def program(nc, x_in, out, w, phases):
    ctx = ExitStack()
    with ctx:
        stack = ctx

        def sb(name, shape, dt=F32):
            return stack.enter_context(nc.sbuf_tensor(name, shape, dt))

        def sem(name):
            return ctx.enter_context(nc.semaphore(name))

        bank = [ctx.enter_context(nc.psum_tensor(f"bank{i}", [P, 512], F32)) for i in range(8)]
        ln_bank = bank[7]

        x_sb = sb("x_sb", [P, SEQS * QT, D])
        ident = sb("ident", [P, P])
        ident_r = sb("ident_r", [P, P], F32R)
        causal = sb("causal", [P, P])
        causal_r = sb("causal_r", [P, P], F32R)
        half_neg = sb("half_neg", [P, QT])
        stats = sb("stats", [P, QT, 6])
        mv = sb("mv", [P, QT, 2])
        var_eps = sb("var_eps", [P, QT])
        rstd = sb("rstd", [P, QT])
        xn = sb("xn", [P, QT, D])
        xh = [sb(f"xh{i}", [P, L], F32R) for i in range(2)]
        xl = [sb(f"xl{i}", [P, L], F32R) for i in range(2)]
        wq_h = sb("wq_h", [P, G * P], F32R)
        wq_l = sb("wq_l", [P, G * P], F32R)
        wkv_h = sb("wkv_h", [P, HG, LD], F32R)
        wkv_l = sb("wkv_l", [P, HG, LD], F32R)
        wvo = sb("wvo", [P, G, D])
        wg_h = sb("wg_h", [P, XP, F], F32R)
        wg_l = sb("wg_l", [P, XP, F], F32R)
        wu_h = sb("wu_h", [P, XP, F], F32R)
        wu_l = sb("wu_l", [P, XP, F], F32R)
        wd_h = sb("wd_h", [P, XP, FC, D], F32R)
        wd_l = sb("wd_l", [P, XP, FC, D], F32R)
        wr_h = sb("wr_h", [P, E], F32R)
        wr_l = sb("wr_l", [P, E], F32R)
        tie = sb("tie", [P, E, E])
        stack = ExitStack()
        wg_st = sb("wg_st", [P, XP, F])
        wu_st = sb("wu_st", [P, XP, F])
        wd_st = sb("wd_st", [P, XP, FC, D])
        wr_st = sb("wr_st", [P, E])
        wkv_st = sb("wkv_st", [P, LD])
        wqT_st = sb("wqT_st", [HD, H, D])
        wkT_st = sb("wkT_st", [HD, H, LD])
        wvT_st = sb("wvT_st", [HD, H, LD])
        wo_st = sb("wo_st", [HD, H, D])
        stack.close()
        stack = ExitStack()
        q_h = sb("q_h", [P, L], F32R)
        q_l = sb("q_l", [P, L], F32R)
        qs = sb("qs", [P, H, L], F32R)
        lat_hi = sb("lat_hi", [P, L], F32R)
        ls = [sb(f"ls{i}", [P, L], F32R) for i in range(2)]
        lat_tok = [sb(f"lat_tok{i}", [P, QT, LD]) for i in range(2)]
        neg_max = sb("neg_max", [P, 2, H, QT])
        row_sum = sb("row_sum", [P, 2, H, QT])
        r_inv = sb("r_inv", [P, HG, QT])
        probs = sb("probs", [P, 3, 512])
        probs_t = sb("probs_t", [P, 2, HG, HEAD_COLS])
        y_t = sb("y_t", [P, L])
        y_q = sb("y_q", [P, QT, HG, LD])
        y_n = sb("y_n", [P, G, L])
        stack.close()
        stack = ExitStack()
        silu_g = sb("silu_g", [P, 2, L])
        hid = sb("hid", [P, 2, L])
        hid_h = [sb(f"hid_h{i}", [P, L], F32R) for i in range(2)]
        hid_l = [sb(f"hid_l{i}", [P, L], F32R) for i in range(2)]
        r_max = sb("r_max", [P, QT])
        r_log = sb("r_log", [P, QT, E])
        r_exp = sb("r_exp", [P, QT, E])
        r_sum = sb("r_sum", [P, QT])
        r_one = sb("r_one", [P, QT])
        score = sb("score", [P, QT, E])
        above = sb("above", [P, QT, E, E])
        equal = sb("equal", [P, QT, E, E])
        rank = sb("rank", [P, QT, E])
        gate = sb("gate", [P, 2, QT, E])
        stack.close()

        stack = ExitStack()
        x_diag = sb("x_diag", [P, QT, CT, SG, CT * HP])
        x_t = sb("x_t", [P, XB, L])
        w_stack = stack
        stack = ExitStack()
        wx_st = sb("wx_st", [P, XB * P])
        wz_st = sb("wz_st", [P, DI + NH])
        stack.close()
        stack = w_stack
        z_s = sb("z_s", [P, QT, DI])
        stack = ExitStack()
        a_cum = sb("a_cum", [P, NC * SG, CH])
        stack.close()
        stack = w_stack
        state = sb("state", [P, NC, DI])
        decay = sb("decay", [P, QT, CT, SG, CH])
        wx_h = sb("wx_h", [P, XB * P], F32R)
        wx_l = sb("wx_l", [P, XB * P], F32R)
        wz_h = sb("wz_h", [P, DI + NH], F32R)
        wz_l = sb("wz_l", [P, DI + NH], F32R)
        w_out = sb("w_out", [P, DI // P, D])
        conv_w = sb("conv_w", [P, XB, TAPS])
        conv_b = sb("conv_b", [P, XB])
        dt_bias = sb("dt_bias", [P, NH])
        neg_a = sb("neg_a", [P, NH])
        y_w = sb("y_w", [P, DI])
        dt_v = sb("dt_v", [P, QT, NH])
        dt_e = sb("dt_e", [P, QT, NH])
        dt_r = sb("dt_r", [P, QT, NH])
        dt_q = sb("dt_q", [P, QT, NH])
        dt_s = sb("dt_s", [P, QT, NH])
        dt_p = sb("dt_p", [P, QT, NH])
        dt = sb("dt", [P, QT, NH])
        a_tok = sb("a_tok", [P, QT, NH])
        a_row = sb("a_row", [P, QT, CT, SG])
        cb = sb("cb", [P, NC, CH])
        b_tok = sb("b_tok", [P, QT, NS])
        x_dt = sb("x_dt", [P, QT, DI])
        x_dec = sb("x_dec", [P, QT, DI])
        e_end = sb("e_end", [P, QT, NH])
        e_cum = sb("e_cum", [P, QT, NH])
        e_tot = sb("e_tot", [P, CT, QT, NH])
        s_dec = sb("s_dec", [P, DI])
        y = sb("y", [P, QT, DI])
        y_stats = sb("y_stats", [P, QT, 6])
        y_mv = sb("y_mv", [P, QT, 2])
        y_var = sb("y_var", [P, QT])
        y_rstd = sb("y_rstd", [P, QT])
        y_ch = sb("y_ch", [P, DI // P, L])
        blocks = sb("blocks", [P, P])
        later = sb("later", [P, P])
        until = sb("until", [P, P])
        until_row = sb("until_row", [P, CH])
        in_chunk = sb("in_chunk", [P, CT, P])
        stack.close()

        s = {n: sem(n) for n in (
            "x0_loaded x_loaded w_loaded c_zero c_made c_round w_hi wfold_mm wfold_hi wfold_done "
            "ln_var ln_eps ln_rstd ln_xn ln_t ln_hi ln_lo xt_free x_done "
            "q_mm q_hi q_lo q_dma s_mm s_max s_exp p_t pt_act pt_dve pv_mm y_ev y_back y_rinv y_norm y_fwd y_ev2 "
            "o_mm stored "
            "m_loaded m_const m_ones m_tri m_hi m_split m_nega m_zeroed xbc_mm conv_step conv_done act_x zdt_mm z_done dt_read dt_step "
            "dt_exp a_done a_rows cum_done xturn_mm xdt_done dec_mm dec_done xdec_done bturn_mm b_done cb_mm cb_done "
            "diff_mm diff_exp mix_done xd_act xd_dve st_mm st_mul st_add yd_mm yo_mm yo_mul y_sum y_mvd y_eps y_pow y_nrm "
            "y_wmul y_zmul yt_mm yt_done so_mm").split()}
        fs = [{n: sem(f"{n}_{f}") for n in (
            "log_mm r_step r_exped gate_mm up_mm silu_done hid_done hid_hi hid_lo down_used down_mm acc_done").split()}
            for f in range(2)]
        block = ctx.enter_context(nc.Block())

        def mm3(pe, o, a_h, a_l, b_h, b_l):
            pe.matmul(o, a_h, b_h, start=True, stop=False)
            pe.matmul(o, a_l, b_h, start=False, stop=False)
            return pe.matmul(o, a_h, b_l, start=False, stop=True)

        LAST = len(phases) - 1
        FN = {ph: sum(p == "ffn" for p in phases[:ph]) for ph in range(len(phases))}
        N_W = 12

        def ln_stats_vector(dve, n, b):
            for t in range(QT):
                dve.bn_stats(stats[:, t, :], x_sb[:, bass.ds(b * QT + t, 1), :].rearrange("p o d -> p (o d)"))
            dve.drain()
            for t in range(QT):
                last = dve.bn_aggr(mv[:, t, :], stats[:, t, :])
            last.then_inc(s["ln_var"], 1)
            dve.wait_ge(s["ln_var"], n + 1)
            dve.tensor_scalar(var_eps[:, :], mv[:, :, 1], LN_EPS, None, ALU.add).then_inc(s["ln_eps"], 1)

        def ln_rstd_gpsimd(pool, n):
            pool.wait_ge(s["ln_eps"], n + 1)
            pool.tensor_tensor(rstd[:, :], var_eps[:, :], half_neg[:, :], ALU.pow).then_inc(s["ln_rstd"], 1)

        def ln_norm_vector(dve, n, b, first=False):
            dve.wait_ge(s["ln_rstd"], n + 1)
            if not first:
                dve.wait_ge(s["ln_t"], n)
            for t in range(QT):
                last = dve.tensor_scalar(xn[:, t, :],
                                         x_sb[:, bass.ds(b * QT + t, 1), :].rearrange("p o d -> p (o d)"),
                                         mv[:, t, 0:1], rstd[:, t:t + 1], ALU.subtract, ALU.mult)
            last.then_inc(s["ln_xn"], 1)

        def ln_turn_tensor(pe, n, first=False):
            pe.wait_ge(s["ln_xn"], n + 1)
            if not first:
                pe.wait_ge(s["ln_lo"], n)
            for t in range(QT):
                last = pe.transpose(ln_bank[:, t * P:(t + 1) * P], xn[:, t, :], ident[:, :])
            last.then_inc(s["ln_t"], 1)

        def ln_hi_scalar(act, n, par, first=False):
            act.wait_ge(s["ln_t"], n + 1)
            if not first:
                act.wait_ge(s["xt_free"], n)
            act.activation(xh[par][:, :], ln_bank[:, :], ACT.Copy).then_inc(s["ln_hi"], 1)

        def ln_lo_vector(dve, n, par):
            dve.wait_ge(s["ln_hi"], n + 1)
            dve.tensor_tensor(xl[par][:, :], ln_bank[:, :], xh[par][:, :], ALU.subtract).then_inc(s["ln_lo"], 1)

        Q_DMAS = 4 * HG
        A_ITEMS = 2 + G

        def proj_tensor(pe, b, par, item, first=False):
            if item == 0:
                pe.wait_ge(s["ln_lo"], b + 1)
            elif item > 0:
                pe.wait_ge(s["q_lo"], b * A_ITEMS + item)
            if item == 0:
                last = mm3(pe, ln_bank[:, :], wkv_h[:, :, :].rearrange("p r c -> p (r c)"),
                           wkv_l[:, :, :].rearrange("p r c -> p (r c)"), xh[par][:, :], xl[par][:, :])
            elif item == 1:
                for t in range(QT):
                    c = slice(t * P, (t + 1) * P)
                    last = mm3(pe, ln_bank[:, t * LD:(t + 1) * LD], xh[par][:, c], xl[par][:, c],
                               wkv_h[:, 0, :], wkv_l[:, 0, :])
            else:
                c = slice((item - 2) * P, (item - 1) * P)
                last = mm3(pe, ln_bank[:, :], wq_h[:, c], wq_l[:, c], xh[par][:, :], xl[par][:, :])
            last.then_inc(s["q_mm"], 1)

        def proj_scalar(act, b, par, item):
            act.wait_ge(s["q_mm"], b * A_ITEMS + item + 1)
            if item == 0:
                act.activation(ls[par][0:64, :], ln_bank[0:64, :], ACT.Copy)
                act.activation(lat_hi[64:128, :], ln_bank[64:128, :], ACT.Copy).then_inc(s["q_hi"], 1)
            elif item == 1:
                act.activation(lat_tok[par][:, :, :], ln_bank[:, 0:QT * LD].rearrange("p (t c) -> p t c", t=QT),
                               ACT.Copy).then_inc(s["q_hi"], 1)
            else:
                g = item - 2
                if not (isinstance(b, int) and b == 0 and g == 0):
                    act.wait_ge(s["q_dma"], (b * G + g) * 16 * Q_DMAS)
                act.activation(q_h[:, :], ln_bank[:, :], ACT.Copy).then_inc(s["q_hi"], 1)

        def proj_vector(dve, b, par, item):
            dve.wait_ge(s["q_hi"], b * A_ITEMS + item + 1)
            if item == 0:
                dve.tensor_tensor(ls[par][64:128, :], ln_bank[64:128, :], lat_hi[64:128, :],
                                  ALU.subtract).then_inc(s["q_lo"], 1)
            elif item == 1:
                dve.sem_inc(s["q_lo"], 1)
            else:
                g = item - 2
                dve.tensor_tensor(q_l[:, :], ln_bank[:, :], q_h[:, :], ALU.subtract).then_inc(s["q_lo"], 1)

        def proj_sync(sp, b, g, first=False):
            parts, used = b * A_ITEMS + 2 + g + 1, (b - 1) * UPS + (g + 1) * HG * UNITS
            if not isinstance(b, int):
                parts, used = sp.to_reg(parts), sp.to_reg(used)
            sp.wait_ge(s["q_lo"], parts)
            if not first:
                sp.wait_ge(s["s_mm"], used)
            for j in range(HG):
                for r, part in enumerate((q_h, q_l, q_h, q_l)):
                    sp.dma_start(qs[r * LD:(r + 1) * LD, g * HG + j, :].bitcast(F32),
                                 part[j * LD:(j + 1) * LD, :].bitcast(F32)).then_inc(s["q_dma"], 16)

        def scores_tensor(pe, b, par, u):
            h, k = divmod(u, UNITS)
            g = h // HG
            o = bank[u % 3]
            if u % (HG * UNITS) == 0:
                pe.wait_ge(s["q_dma"], (b * G + g + 1) * 16 * Q_DMAS)
            if not (isinstance(b, int) and b == 0 and u < 3):
                pe.wait_ge(s["s_exp"], b * UPS + u - 2)
            for qt, at in UNIT_TILES[k]:
                n = (qt + 1) * P
                q = qs[:, h, qt * P:(qt + 1) * P]
                pe.matmul(o[:, at:at + n], q, ls[par][:, 0:n], start=(at == 0), stop=False, skip_group_check=True)
                last = pe.matmul(o[:, at + qt * P:at + n], ident_r[:, :], causal_r[:, :], start=False, stop=True,
                                 skip_group_check=True)
            last.then_inc(s["s_mm"], 1)

        def max_vector(dve, b, par, u):
            h, k = divmod(u, UNITS)
            dve.wait_ge(s["s_mm"], b * UPS + u + 1)
            for qt, at in UNIT_TILES[k]:
                last = dve.tensor_reduce(neg_max[:, par, h, qt:qt + 1], bank[u % 3][:, at:at + (qt + 1) * P], AX.X,
                                         ALU.max, negate=True)
            last.then_inc(s["s_max"], 1)

        def exp_scalar(act, b, par, u):
            h, k = divmod(u, UNITS)
            act.wait_ge(s["s_max"], b * UPS + u + 1)
            if not (isinstance(b, int) and b == 0 and u < 3):
                act.wait_ge(s["p_t"], b * UPS + u - 2)
            for qt, at in UNIT_TILES[k]:
                c = slice(at, at + (qt + 1) * P)
                last = act.activation(probs[:, u % 3, c], bank[u % 3][:, c], ACT.Exp,
                                      bias=neg_max[:, par, h, qt:qt + 1], accum_out=row_sum[:, par, h, qt:qt + 1])
            last.then_inc(s["s_exp"], 1)

        def turn_tensor(pe, b, u):
            k = u % UNITS
            pe.wait_ge(s["s_exp"], b * UPS + u + 1)
            if not (isinstance(b, int) and b == 0 and u < 2):
                pe.wait_ge(s["pt_act" if u % 2 == 0 else "pt_dve"], b * (UPS // 2) + u // 2)
            for c in range(0, UNIT_COLS[k], P):
                last = pe.transpose(bank[3 + u % 2][:, c:c + P], probs[:, u % 3, c:c + P], ident[:, :])
            last.then_inc(s["p_t"], 1)

        def turned_copy(eng, b, u):
            h, k = divmod(u, UNITS)
            g = h // HG
            eng.wait_ge(s["p_t"], b * UPS + u + 1)
            if u % (HG * UNITS) < 2 and not (isinstance(b, int) and b == 0 and g < 2):
                eng.wait_ge(s["pv_mm"], b * G + g - 1)
            o = probs_t[:, g % 2, h % HG, UNIT_AT[k]:UNIT_AT[k] + UNIT_COLS[k]]
            i = bank[3 + u % 2][:, 0:UNIT_COLS[k]]
            return o, i

        def turned_scalar(act, b, u):
            o, i = turned_copy(act, b, u)
            act.activation(o, i, ACT.Copy).then_inc(s["pt_act"], 1)

        def turned_vector(dve, b, u):
            o, i = turned_copy(dve, b, u)
            dve.tensor_copy(o, i).then_inc(s["pt_dve"], 1)

        def values_tensor(pe, b, par, g):
            pe.wait_ge(s["pt_act"], b * (UPS // 2) + (g + 1) * HG * UNITS // 2)
            pe.wait_ge(s["pt_dve"], b * (UPS // 2) + (g + 1) * HG * UNITS // 2)
            if not (isinstance(b, int) and b == 0 and g == 0):
                pe.wait_ge(s["y_ev"], b * G + g)
                if g == 0:
                    pe.wait_ge(s["x_done"], b)
            first = [True] * HG
            for k in range(UNITS):
                for qt, at in UNIT_TILES[k]:
                    for kb in range(qt + 1):
                        for j in range(HG):
                            c = UNIT_AT[k] + at + kb * P
                            last = pe.matmul(bank[5][j * LD:(j + 1) * LD, qt * P:(qt + 1) * P], lat_tok[par][:, kb, :],
                                             probs_t[:, g % 2, j, c:c + P], start=first[j], stop=(kb == qt),
                                             skip_group_check=True)
                            if g == G - 1 and first[j] and j == 0:
                                last.then_inc(s["xt_free"], 1)
                            first[j] = False
            last.then_inc(s["pv_mm"], 1)

        def y_copy_scalar(act, b, g):
            act.wait_ge(s["pv_mm"], b * G + g + 1)
            if not (isinstance(b, int) and b == 0 and g == 0):
                act.wait_ge(s["y_back"], b * G + g)
            act.activation(y_t[:, :], bank[5][:, :], ACT.Copy).then_inc(s["y_ev"], 1)

        def y_back_tensor(pe, b, g):
            pe.wait_ge(s["y_ev"], b * G + g + 1)
            if not (isinstance(b, int) and b == 0 and g == 0):
                pe.wait_ge(s["y_ev2"], b * G + g)
            for t in range(QT):
                last = pe.transpose(bank[6][:, t * P:(t + 1) * P], y_t[:, t * P:(t + 1) * P], ident[:, :])
            last.then_inc(s["y_back"], 1)

        def y_norm_vector(dve, b, par, g):
            dve.wait_ge(s["s_exp"], b * UPS + (g + 1) * HG * UNITS)
            dve.reciprocal(r_inv[:, :, :], row_sum[:, par, g * HG:(g + 1) * HG, :]).then_inc(s["y_rinv"], 1)
            dve.wait_ge(s["y_rinv"], b * G + g + 1)
            dve.wait_ge(s["y_back"], b * G + g + 1)
            if not (isinstance(b, int) and b == 0 and g == 0):
                dve.wait_ge(s["y_fwd"], b * G + g)
            dve.tensor_tensor(y_q[:, :, :, :], bank[6][:, :].rearrange("p (t j c) -> p t j c", t=QT, j=HG),
                              r_inv[:, :, :].rearrange("p j (t o) -> p t j o", o=1).to_broadcast([P, QT, HG, LD]),
                              ALU.mult).then_inc(s["y_norm"], 1)

        def y_fwd_tensor(pe, b, g):
            pe.wait_ge(s["y_norm"], b * G + g + 1)
            for t in range(QT):
                last = pe.transpose(bank[6][:, t * P:(t + 1) * P], y_q[:, t, :, :].rearrange("p j c -> p (j c)"),
                                    ident[:, :])
            last.then_inc(s["y_fwd"], 1)

        def y_copy2_scalar(act, b, g):
            act.wait_ge(s["y_fwd"], b * G + g + 1)
            if g == 0 and not (isinstance(b, int) and b == 0):
                act.wait_ge(s["o_mm"], b)
            act.activation(y_n[:, g, :], bank[6][:, :], ACT.Copy).then_inc(s["y_ev2"], 1)

        def out_tensor(pe, b):
            pe.wait_ge(s["y_ev2"], b * G + G)
            for t in range(QT):
                for g in range(G):
                    last = pe.matmul(bank[5][:, t * P:(t + 1) * P], y_n[:, g, t * P:(t + 1) * P], wvo[:, g, :],
                                     start=(g == 0), stop=(g == G - 1))
            last.then_inc(s["o_mm"], 1)

        def out_vector(dve, b):
            dve.wait_ge(s["o_mm"], b + 1)
            xv = x_sb[:, bass.ds(b * QT, QT), :]
            dve.tensor_tensor(xv, bank[5][:, :].rearrange("p (t d) -> p t d", t=QT), xv,
                              ALU.add).then_inc(s["x_done"], 1)

        GU = HG * UNITS
        LN_AT = {"stats": 2, "norm": 5, "turn": 8, "hi": 9, "lo": 10}
        PROJ_AT = [14 + 4 * i for i in range(A_ITEMS)]

        def attn_tensor(pe):
            def batch(b, par, nxt, proj):
                scores_tensor(pe, b, par, 0)
                scores_tensor(pe, b, par, 1)
                for u in range(UPS):
                    if u + 2 < UPS:
                        scores_tensor(pe, b, par, u + 2)
                    turn_tensor(pe, b, u)
                    g, v = divmod(u, GU)
                    if g and v == 3:
                        values_tensor(pe, b, par, g - 1)
                    if g and v == 6:
                        y_back_tensor(pe, b, g - 1)
                    if g and v == 9:
                        y_fwd_tensor(pe, b, g - 1)
                    if u == LN_AT["turn"]:
                        ln_turn_tensor(pe, b + 1)
                    if proj and u in PROJ_AT:
                        proj_tensor(pe, b + 1, 1 - par, PROJ_AT.index(u))
                values_tensor(pe, b, par, G - 1)
                y_back_tensor(pe, b, G - 1)
                y_fwd_tensor(pe, b, G - 1)
                out_tensor(pe, b)

            for item in range(A_ITEMS):
                proj_tensor(pe, 0, 0, item)
            with_pairs(pe, batch)

        def attn_vector(dve):
            def batch(b, par, nxt, proj):
                for u in range(UPS):
                    max_vector(dve, b, par, u)
                    if u and (u - 1) % 2:
                        turned_vector(dve, b, u - 1)
                    g, v = divmod(u, GU)
                    if g and v == 7:
                        y_norm_vector(dve, b, par, g - 1)
                    if u == LN_AT["stats"]:
                        ln_stats_vector(dve, b + 1, nxt)
                    if u == LN_AT["norm"]:
                        ln_norm_vector(dve, b + 1, nxt)
                    if u == LN_AT["lo"]:
                        ln_lo_vector(dve, b + 1, 1 - par)
                    if proj and u - 1 in PROJ_AT:
                        proj_vector(dve, b + 1, 1 - par, PROJ_AT.index(u - 1))
                turned_vector(dve, b, UPS - 1)
                y_norm_vector(dve, b, par, G - 1)
                out_vector(dve, b)

            for item in range(A_ITEMS):
                proj_vector(dve, 0, 0, item)
            with_pairs(dve, batch)

        def attn_scalar(act):
            def batch(b, par, nxt, proj):
                for u in range(UPS):
                    exp_scalar(act, b, par, u)
                    if u and (u - 1) % 2 == 0:
                        turned_scalar(act, b, u - 1)
                    g, v = divmod(u, GU)
                    if g and v == 5:
                        y_copy_scalar(act, b, g - 1)
                    if g and v == 10:
                        y_copy2_scalar(act, b, g - 1)
                    if u == LN_AT["hi"]:
                        ln_hi_scalar(act, b + 1, 1 - par)
                    if proj and u - 1 in PROJ_AT:
                        proj_scalar(act, b + 1, 1 - par, PROJ_AT.index(u - 1))
                y_copy_scalar(act, b, G - 1)
                y_copy2_scalar(act, b, G - 1)

            for item in range(A_ITEMS):
                proj_scalar(act, 0, 0, item)
            with_pairs(act, batch)

        def attn_gpsimd(pool):
            def batch(b, par, nxt, proj):
                ln_rstd_gpsimd(pool, b + 1)
            with_pairs(pool, batch)

        def attn_sync(sp):
            def batch(b, par, nxt, proj):
                if proj:
                    for g in range(G):
                        proj_sync(sp, b + 1, g)
            for g in range(G):
                proj_sync(sp, 0, g, first=True)
            with_pairs(sp, batch)

        def with_pairs(eng, batch):
            batch(0, 0, 1, True)
            batch(1, 1, 2, True)
            with eng.Fori(1, PAIRS - 1) as i:
                batch(2 * i, 0, 2 * i + 1, True)
                batch(2 * i + 1, 1, 2 * i + 2, True)
            batch(SEQS - 2, 0, SEQS - 1, True)
            batch(SEQS - 1, 1, 0, False)

        R_STEPS = 12

        def route_tensor(pe, f, b, par, n):
            z = fs[f]
            pe.wait_ge(s["ln_lo"], n + 1)
            if not (isinstance(b, int) and b == 0):
                pe.wait_ge(z["r_step"], (b - 1) * R_STEPS + 2)
            for t in range(QT):
                c = slice(t * P, (t + 1) * P)
                last = mm3(pe, bank[6][:, t * E:(t + 1) * E], xh[par][:, c], xl[par][:, c], wr_h[:, :], wr_l[:, :])
            last.then_inc(z["log_mm"], 1)

        def route_a_vector(dve, f, b):
            z = fs[f]
            logits = bank[6][:, 0:QT * E].rearrange("p (t e) -> p t e", t=QT)
            n = b * R_STEPS
            dve.wait_ge(z["log_mm"], b + 1)
            dve.tensor_reduce(r_max[:, :], logits, AX.X, ALU.max).then_inc(z["r_step"], 1)
            dve.wait_ge(z["r_step"], n + 1)
            dve.tensor_tensor(r_log[:, :, :], logits,
                              r_max[:, :].rearrange("p (t o) -> p t o", o=1).to_broadcast([P, QT, E]),
                              ALU.subtract).then_inc(z["r_step"], 1)

        def route_scalar(act, f, b):
            z = fs[f]
            act.wait_ge(z["r_step"], b * R_STEPS + 2)
            act.activation(r_exp[:, :, :], r_log[:, :, :], ACT.Exp).then_inc(z["r_exped"], 1)

        def route_b_vector(dve, f, b, par):
            z = fs[f]
            n = b * R_STEPS
            dve.wait_ge(z["r_exped"], b + 1)
            dve.tensor_reduce(r_sum[:, :], r_exp[:, :, :], AX.X, ALU.add).then_inc(z["r_step"], 1)
            dve.wait_ge(z["r_step"], n + 3)
            dve.reciprocal(r_one[:, :], r_sum[:, :]).then_inc(z["r_step"], 1)
            dve.wait_ge(z["r_step"], n + 4)
            dve.tensor_tensor(score[:, :, :], r_exp[:, :, :],
                              r_one[:, :].rearrange("p (t o) -> p t o", o=1).to_broadcast([P, QT, E]),
                              ALU.mult).then_inc(z["r_step"], 1)
            dve.wait_ge(z["r_step"], n + 5)
            for t in range(QT):
                other = score[:, t, :].rearrange("p (o j) -> p o j", o=1).to_broadcast([P, E, E])
                own = score[:, t, :].rearrange("p (e o) -> p e o", o=1).to_broadcast([P, E, E])
                dve.tensor_tensor(above[:, t, :, :], other, own, ALU.is_gt)
                last = dve.tensor_tensor(equal[:, t, :, :], other, own, ALU.is_equal)
            last.then_inc(z["r_step"], 1)
            dve.wait_ge(z["r_step"], n + 6)
            for t in range(QT):
                last = dve.tensor_tensor(equal[:, t, :, :], equal[:, t, :, :], tie[:, :, :], ALU.mult)
            last.then_inc(z["r_step"], 1)
            dve.wait_ge(z["r_step"], n + 7)
            dve.tensor_tensor(above[:, :, :, :].rearrange("p t e j -> p (t e j)"),
                              above[:, :, :, :].rearrange("p t e j -> p (t e j)"),
                              equal[:, :, :, :].rearrange("p t e j -> p (t e j)"), ALU.add).then_inc(z["r_step"], 1)
            dve.wait_ge(z["r_step"], n + 8)
            dve.tensor_reduce(rank[:, :, :], above[:, :, :, :], AX.X, ALU.add).then_inc(z["r_step"], 1)
            dve.wait_ge(z["r_step"], n + 9)
            dve.scalar_tensor_tensor(out=score[:, :, :], in0=rank[:, :, :], scalar=TOPK - 0.5, in1=score[:, :, :],
                                     op0=ALU.is_lt, op1=ALU.mult).then_inc(z["r_step"], 1)
            dve.wait_ge(z["r_step"], n + 10)
            dve.tensor_reduce(r_sum[:, :], score[:, :, :], AX.X, ALU.add).then_inc(z["r_step"], 1)
            dve.wait_ge(z["r_step"], n + 11)
            dve.tensor_scalar(r_max[:, :], r_sum[:, :], ROUTE_EPS, None, ALU.add).then_inc(z["r_step"], 1)
            dve.wait_ge(z["r_step"], n + 12)
            dve.reciprocal(r_one[:, :], r_max[:, :]).then_inc(z["log_read"], 1)
            dve.wait_ge(z["log_read"], b + 1)
            dve.tensor_tensor(gate[:, par, :, :], score[:, :, :],
                              r_one[:, :].rearrange("p (t o) -> p t o", o=1).to_broadcast([P, QT, E]),
                              ALU.mult).then_inc(z["gated"], 1)

        for f in range(2):
            fs[f]["log_read"] = sem(f"log_read_{f}")
            fs[f]["gated"] = sem(f"gated_{f}")

        def hidden_tensor(pe, f, b, par, k):
            z, m = fs[f], b * MU + k
            e, c = divmod(k, FC)
            cols = slice(c * P, (c + 1) * P)
            static_first = isinstance(b, int) and b == 0 and k < 2
            if not static_first:
                pe.wait_ge(z["silu_done"], m - 1)
            mm3(pe, bank[k % 2][:, :], wg_h[:, e, cols], wg_l[:, e, cols], xh[par][:, :],
                xl[par][:, :]).then_inc(z["gate_mm"], 1)
            if not static_first:
                pe.wait_ge(z["hid_done"], m - 1)
            last = mm3(pe, bank[2 + k % 2][:, :], wu_h[:, e, cols], wu_l[:, e, cols], xh[par][:, :], xl[par][:, :])
            last.then_inc(z["up_mm"], 1)

        def down_tensor(pe, f, b, par, k):
            z, m = fs[f], b * MU + k
            e, c = divmod(k, FC)
            o = bank[4 + (par * XP + e) % 2]
            if c == 0 and not (isinstance(b, int) and b == 0 and e < 2):
                pe.wait_ge(z["acc_done"], b * XP + e - 1)
            pe.wait_ge(z["hid_lo"], m + 1)
            for t in range(QT):
                cols = slice(t * P, (t + 1) * P)
                a_h, a_l = hid_h[k % 2][:, cols], hid_l[k % 2][:, cols]
                b_h, b_l = wd_h[:, e, c, :], wd_l[:, e, c, :]
                mm = pe.matmul(o[:, cols], a_h, b_h, start=(c == 0 and t == 0), stop=False, skip_group_check=True)
                if k == MU - 1 and t == 0:
                    mm.then_inc(s["xt_free"], 1)
                pe.matmul(o[:, cols], a_l, b_h, start=False, stop=False, skip_group_check=True)
                last = pe.matmul(o[:, cols], a_h, b_l, start=False, stop=(c == FC - 1), skip_group_check=True)
            last.then_inc(z["down_used"], 1)

        def silu_scalar(act, f, b, k):
            z, m = fs[f], b * MU + k
            act.wait_ge(z["gate_mm"], m + 1)
            if not (isinstance(b, int) and b == 0 and k < 2):
                act.wait_ge(z["hid_done"], m - 1)
            act.activation(silu_g[:, k % 2, :], bank[k % 2][:, :], ACT.Silu).then_inc(z["silu_done"], 1)

        def hid_vector(dve, f, b, k):
            z, m = fs[f], b * MU + k
            dve.wait_ge(z["silu_done"], m + 1)
            dve.wait_ge(z["up_mm"], m + 1)
            if not (isinstance(b, int) and b == 0 and k < 2):
                dve.wait_ge(z["hid_lo"], m - 1)
            dve.tensor_tensor(hid[:, k % 2, :], bank[2 + k % 2][:, :], silu_g[:, k % 2, :],
                              ALU.mult).then_inc(z["hid_done"], 1)

        def hid_hi_scalar(act, f, b, k):
            z, m = fs[f], b * MU + k
            act.wait_ge(z["hid_done"], m + 1)
            if not (isinstance(b, int) and b == 0 and k < 2):
                act.wait_ge(z["down_used"], m - 1)
            act.activation(hid_h[k % 2][:, :], hid[:, k % 2, :], ACT.Copy).then_inc(z["hid_hi"], 1)

        def hid_lo_gpsimd(pool, f, b, k):
            z, m = fs[f], b * MU + k
            pool.wait_ge(z["hid_hi"], m + 1)
            pool.tensor_tensor(hid_l[k % 2][:, :], hid[:, k % 2, :], hid_h[k % 2][:, :],
                               ALU.subtract).then_inc(z["hid_lo"], 1)

        def add_vector(dve, f, b, par, e):
            z = fs[f]
            o = bank[4 + (par * XP + e) % 2]
            dve.wait_ge(z["down_used"], b * MU + (e + 1) * FC)
            if e == 0:
                xv = x_sb[:, bass.ds(b * QT, QT), :]
                dve.tensor_tensor(xv, o[:, :].rearrange("p (t d) -> p t d", t=QT), xv,
                                  ALU.add).then_inc(z["acc_done"], 1)
                return
            if e == 1:
                dve.wait_ge(z["gated"], b + 1)
            dve.wait_ge(z["acc_done"], b * XP + e)
            for t in range(QT):
                xt = x_sb[:, bass.ds(b * QT + t, 1), :].rearrange("p o d -> p (o d)")
                last = dve.scalar_tensor_tensor(out=xt, in0=o[:, t * P:(t + 1) * P], scalar=gate[:, par, t, e - 1:e],
                                                in1=xt, op0=ALU.mult, op1=ALU.add)
            last.then_inc(z["acc_done"], 1)

        F_LN = {"stats": 3, "norm": 5, "turn": 7, "hi": 8, "lo": 9, "route": 10, "route_a": 11, "route_b": 13}

        def ffn_tensor(pe, f, ph):
            def batch(b, par, nxt, more):
                n = ph * SEQS + b
                for k in range(MU):
                    hidden_tensor(pe, f, b, par, k)
                    if k >= 2:
                        down_tensor(pe, f, b, par, k - 2)
                    if k == F_LN["turn"] and (more or ph < LAST):
                        ln_turn_tensor(pe, n + 1)
                    if k == F_LN["route"] and more:
                        route_tensor(pe, f, b + 1, 1 - par, n + 1)
                down_tensor(pe, f, b, par, MU - 2)
                down_tensor(pe, f, b, par, MU - 1)
            if ph:
                pe.wait_ge(s["x_done"], ph * SEQS)
            route_tensor(pe, f, 0, 0, ph * SEQS)
            with_pairs(pe, batch)

        def ffn_vector(dve, f, ph):
            def batch(b, par, nxt, more):
                n = ph * SEQS + b
                for k in range(MU):
                    hid_vector(dve, f, b, k)
                    if k >= 4 and k % 2 == 0:
                        add_vector(dve, f, b, par, k // 2 - 2)
                    if more or ph < LAST:
                        if k == F_LN["stats"]:
                            ln_stats_vector(dve, n + 1, nxt)
                        if k == F_LN["norm"]:
                            ln_norm_vector(dve, n + 1, nxt)
                        if k == F_LN["lo"]:
                            ln_lo_vector(dve, n + 1, 1 - par)
                    if more and k == F_LN["route_a"]:
                        route_a_vector(dve, f, b + 1)
                    if more and k == F_LN["route_b"]:
                        route_b_vector(dve, f, b + 1, 1 - par)
                for e in range(XP - 2, XP):
                    add_vector(dve, f, b, par, e)
                dve.wait_ge(fs[f]["acc_done"], b * XP + XP)
                dve.sem_inc(s["x_done"], 1)
            if ph:
                dve.wait_ge(s["x_done"], ph * SEQS)
            route_a_vector(dve, f, 0)
            route_b_vector(dve, f, 0, 0)
            with_pairs(dve, batch)

        def ffn_scalar(act, f, ph):
            def batch(b, par, nxt, more):
                n = ph * SEQS + b
                for k in range(MU):
                    silu_scalar(act, f, b, k)
                    if k:
                        hid_hi_scalar(act, f, b, k - 1)
                    if k == F_LN["hi"] and (more or ph < LAST):
                        ln_hi_scalar(act, n + 1, 1 - par)
                    if more and k == F_LN["route_a"]:
                        route_scalar(act, f, b + 1)
                hid_hi_scalar(act, f, b, MU - 1)
            route_scalar(act, f, 0)
            with_pairs(act, batch)

        def ffn_gpsimd(pool, f, ph):
            def batch(b, par, nxt, more):
                n = ph * SEQS + b
                for k in range(MU):
                    hid_lo_gpsimd(pool, f, b, k)
                    if k == F_LN["stats"] - 1 and (more or ph < LAST):
                        ln_rstd_gpsimd(pool, n + 1)
            with_pairs(pool, batch)

        def flat_t(t):
            return t[:, :, :].rearrange("p t h -> p (t h)")

        def ssm_tensor(pe, ph):
            def batch(b, par, nxt, more):
                static0 = isinstance(b, int) and b == 0
                n = ph * SEQS + b
                if not static0:
                    pe.wait_ge(s["yo_mul"], b * 2)
                    pe.wait_ge(s["y_sum"], b * 2)
                for q in range(XB):
                    c = slice(q * P, (q + 1) * P)
                    mm3(pe, bank[q][:, :], wx_h[:, c], wx_l[:, c], xh[par][:, :],
                        xl[par][:, :]).then_inc(s["xbc_mm"], 1)
                for t in range(QT):
                    c = slice(t * P, (t + 1) * P)
                    if t >= 2:
                        pe.wait_ge(s["dt_read"], b * QT + t - 1)
                    elif not static0:
                        pe.wait_ge(s["yt_done"], b * 2)
                    mm3(pe, bank[4 + t % 2][:, 0:DI + NH], xh[par][:, c], xl[par][:, c], wz_h[:, :],
                        wz_l[:, :]).then_inc(s["zdt_mm"], 1)
                pe.wait_ge(s["act_x"], b * XB + XB)
                for t in range(QT):
                    for q in range(DI // P):
                        last = pe.transpose(bank[t // 2][:, (t % 2) * DI + q * P:(t % 2) * DI + (q + 1) * P],
                                            x_t[:, q, t * P:(t + 1) * P], ident[:, :])
                    if t == 0:
                        last.then_inc(s["xt_free"], 1)
                last.then_inc(s["xturn_mm"], 1)
                for t in range(QT):
                    last = pe.transpose(bank[2][:, t * P:(t + 1) * P], x_t[:, 2, t * P:(t + 1) * P], ident[:, :])
                last.then_inc(s["bturn_mm"], 1)
                for ch in range(NC):
                    c = slice(ch * CH, (ch + 1) * CH)
                    for r in range(CT):
                        last = pe.matmul(bank[3][r * CH:(r + 1) * CH, c], x_t[:, 2, c], x_t[:, 3, c], start=True, stop=True)
                last.then_inc(s["cb_mm"], 1)
                pe.wait_ge(s["a_done"], b + 1)
                pe.wait_ge(s["z_done"], b * QT + QT)
                pe.matmul(bank[4][:, 0:QT * NH], later[:, :], flat_t(a_tok), start=True, stop=True)
                pe.matmul(bank[4][:, QT * NH:2 * QT * NH], until[:, :], flat_t(a_tok), start=True, stop=True)
                for c in range(CT):
                    last = pe.matmul(bank[5][:, c * QT * NH:(c + 1) * QT * NH], in_chunk[:, c, :], flat_t(a_tok),
                                     start=True, stop=True)
                last.then_inc(s["dec_mm"], 1)
                pe.wait_ge(s["cum_done"], b + 1)
                pe.wait_ge(s["xdt_done"], b + 1)
                cum = a_cum[:, :, :].rearrange("p g l -> p (g l)")
                for i in range(NC * SG * CH // 512):
                    if i >= 2:
                        pe.wait_ge(s["diff_exp"], b * 8 + i - 1)
                    pe.matmul(bank[i % 2][:, :], later[:, :], cum[:, i * 512:(i + 1) * 512], start=True,
                              stop=True).then_inc(s["diff_mm"], 1)
                pe.wait_ge(s["mix_done"], b * 4 + 4)
                pe.wait_ge(s["xd_act"], b + 1)
                pe.wait_ge(s["xd_dve"], b + 1)
                pe.wait_ge(s["b_done"], b + 1)
                for t in range(QT):
                    for g in range(SG):
                        for c in range(CT):
                            o = bank[2 + t // 2][c * CH:(c + 1) * CH, (t % 2) * DI + g * CH:(t % 2) * DI + (g + 1) * CH]
                            last = pe.matmul(o, decay[:, t, c, g, :], x_diag[:, t, c, g, :], start=True, stop=True)
                last.then_inc(s["yd_mm"], 1)
                pe.wait_ge(s["xdec_done"], b + 1)
                pe.wait_ge(s["dec_done"], b * 3 + 3)
                for ch in range(NC - 1):
                    t, c = divmod(ch, CT)
                    rows = slice(c * CH, (c + 1) * CH)
                    if ch >= 2:
                        pe.wait_ge(s["st_add"], b * (NC - 1) + ch - 1)
                    pe.matmul(bank[4 + ch % 2][:, 0:DI], b_tok[rows, t, :], x_dec[rows, t, :], start=True,
                              stop=True).then_inc(s["st_mm"], 1)
                if more or ph < LAST:
                    ln_turn_tensor(pe, n + 1)
                pe.wait_ge(s["diff_exp"], b * 8 + 8)
                for ch in range(NC):
                    t, c = divmod(ch, CT)
                    pe.wait_ge(s["st_add"], b * (NC - 1) + max(ch, 1))
                    last = pe.matmul(bank[t // 2][c * CH:(c + 1) * CH, (t % 2) * DI:(t % 2 + 1) * DI],
                                     x_t[:, 3, ch * CH:(ch + 1) * CH], state[:, ch, :], start=True, stop=True)
                last.then_inc(s["yo_mm"], 1)
                pe.wait_ge(s["y_zmul"], b + 1)
                for q in range(DI // P):
                    for t in range(QT):
                        last = pe.transpose(bank[4 + q][:, t * P:(t + 1) * P], y[:, t, q * P:(q + 1) * P], ident[:, :])
                last.then_inc(s["yt_mm"], 1)
                pe.wait_ge(s["yt_done"], b * 2 + 2)
                if not static0:
                    pe.wait_ge(s["x_done"], n)
                for t in range(QT):
                    for q in range(DI // P):
                        last = pe.matmul(bank[6][:, t * D:(t + 1) * D], y_ch[:, q, t * P:(t + 1) * P], w_out[:, q, :],
                                         start=(q == 0), stop=(q == DI // P - 1))
                last.then_inc(s["so_mm"], 1)
            pe.wait_ge(s["m_split"], 1)
            pe.wait_ge(s["m_const"], 1)
            with_pairs(pe, batch)

        def ssm_vector(dve, ph):
            dve.wait_ge(s["x_done"], ph * SEQS)
            dve.wait_ge(s["m_hi"], 1)
            dve.tensor_tensor(wx_l[:, :], wx_st[:, :], wx_h[:, :], ALU.subtract)
            dve.tensor_tensor(wz_l[:, :], wz_st[:, :], wz_h[:, :], ALU.subtract).then_inc(s["m_split"], 1)
            dve.tensor_scalar(neg_a[:, :], neg_a[:, :], -1.0, None, ALU.mult).then_inc(s["m_nega"], 1)
            dve.memset(x_diag[:, :, :, :, :].rearrange("p t c g x -> p (t c g x)"), 0.0).then_inc(s["m_zeroed"], 1)
            dve.wait_ge(s["m_zeroed"], 1)
            dve.wait_ge(s["m_nega"], 1)
            dve.wait_ge(s["m_const"], 1)

            def batch(b, par, nxt, more):
                static0 = isinstance(b, int) and b == 0
                n = ph * SEQS + b
                for q in range(XB):
                    dve.wait_ge(s["xbc_mm"], b * XB + q + 1)
                    if q == 0 and not static0:
                        dve.wait_ge(s["yo_mm"], b)
                    dve.tensor_scalar(x_t[:, q, :], bank[q][:, :], conv_w[:, q, TAPS - 1:TAPS], conv_b[:, q:q + 1],
                                      ALU.mult, ALU.add).then_inc(s["conv_step"], 1)
                    for k in range(1, TAPS):
                        dve.wait_ge(s["conv_step"], (b * XB + q) * TAPS + k)
                        dve.scalar_tensor_tensor(out=x_t[:, q, k:L], in0=bank[q][:, 0:L - k],
                                                 scalar=conv_w[:, q, TAPS - 1 - k:TAPS - k], in1=x_t[:, q, k:L],
                                                 op0=ALU.mult, op1=ALU.add).then_inc(s["conv_step"], 1)
                for t in range(QT):
                    dve.wait_ge(s["z_done"], b * QT + t + 1)
                    dve.tensor_tensor(dt_v[:, t, :], bank[4 + t % 2][:, DI:DI + NH], dt_bias[:, :],
                                      ALU.add).then_inc(s["dt_read"], 1)
                dve.wait_ge(s["dt_read"], b * QT + QT)
                steps = b * DT_STEPS

                def step(r):
                    dve.wait_ge(s["dt_step"], steps + r)

                dve.tensor_scalar(dt_r[:, :, :], dt_v[:, :, :], 0.0, None, ALU.max).then_inc(s["dt_step"], 1)
                step(1)
                dve.scalar_tensor_tensor(out=dt_s[:, :, :], in0=dt_r[:, :, :], scalar=2.0, in1=dt_v[:, :, :],
                                         op0=ALU.mult, op1=ALU.subtract).then_inc(s["dt_step"], 1)
                dve.wait_ge(s["dt_exp"], b + 1)
                dve.tensor_scalar(dt_q[:, :, :], dt_e[:, :, :], 2.0, None, ALU.add).then_inc(s["dt_step"], 1)
                step(3)
                dve.reciprocal(dt_p[:, :, :], dt_q[:, :, :]).then_inc(s["dt_step"], 1)
                step(4)
                dve.tensor_tensor(dt_q[:, :, :], dt_e[:, :, :], dt_p[:, :, :], ALU.mult).then_inc(s["dt_step"], 1)
                step(5)
                dve.tensor_tensor(dt_s[:, :, :], dt_q[:, :, :], dt_q[:, :, :], ALU.mult).then_inc(s["dt_step"], 1)
                step(6)
                dve.tensor_scalar(dt_p[:, :, :], dt_s[:, :, :], ATANH[0], None, ALU.mult).then_inc(s["dt_step"], 1)
                r = 7
                for coefficient in ATANH[1:]:
                    step(r)
                    dve.scalar_tensor_tensor(out=dt_p[:, :, :], in0=dt_p[:, :, :], scalar=coefficient, in1=dt_s[:, :, :],
                                             op0=ALU.add, op1=ALU.mult).then_inc(s["dt_step"], 1)
                    r += 1
                step(r)
                dve.scalar_tensor_tensor(out=dt_p[:, :, :], in0=dt_p[:, :, :], scalar=1.0, in1=dt_q[:, :, :], op0=ALU.add,
                                         op1=ALU.mult).then_inc(s["dt_step"], 1)
                step(r + 1)
                dve.scalar_tensor_tensor(out=dt[:, :, :], in0=dt_p[:, :, :], scalar=2.0, in1=dt_r[:, :, :], op0=ALU.mult,
                                         op1=ALU.add).then_inc(s["dt_step"], 1)
                step(r + 2)
                assert r + 2 == DT_STEPS
                dve.tensor_tensor(a_tok[:, :, :], dt[:, :, :],
                                  neg_a[:, :].rearrange("p (o h) -> p o h", o=1).to_broadcast([P, QT, NH]),
                                  ALU.mult).then_inc(s["a_done"], 1)
                dve.wait_ge(s["a_done"], b + 1)
                for c in range(CT):
                    for j in range(CT):
                        last = dve.tensor_copy(a_row[j * CH:(j + 1) * CH, :, c, :],
                                               a_tok[c * CH:(c + 1) * CH, :, :].rearrange("p t (g j) -> p t g j",
                                                                                         j=CT)[:, :, :, j])
                last.then_inc(s["a_rows"], 1)
                dve.wait_ge(s["a_rows"], b + 1)
                if not static0:
                    dve.wait_ge(s["yo_mm"], b)
                dve.tensor_tensor(a_cum[:, :, :],
                                  a_row[:, :, :, :].rearrange("p t c (g o) -> p (t c g) o", o=1)
                                  .to_broadcast([P, NC * SG, CH]),
                                  until_row[:, :].rearrange("p (o l) -> p o l", o=1).to_broadcast([P, NC * SG, CH]),
                                  ALU.mult).then_inc(s["cum_done"], 1)
                dve.wait_ge(s["xturn_mm"], b + 1)
                for i in range(QT // 2):
                    last = dve.tensor_tensor(
                        x_dt[:, 2 * i:2 * i + 2, :].rearrange("p t (h c) -> p (t h) c", c=HP),
                        bank[i][:, :].rearrange("p (h c) -> p h c", c=HP),
                        dt[:, 2 * i:2 * i + 2, :].rearrange("p t (h o) -> p (t h) o", o=1).to_broadcast([P, 2 * NH, HP]),
                        ALU.mult)
                last.then_inc(s["xdt_done"], 1)
                dve.wait_ge(s["xdt_done"], b + 1)
                for c in range(CT // 2, CT):
                    for j in range(CT):
                        last = dve.tensor_copy(
                            x_diag[j * CH:(j + 1) * CH, :, c, :, j * HP:(j + 1) * HP],
                            x_dt[c * CH:(c + 1) * CH, :, :].rearrange("p t (g j x) -> p t g j x", g=SG, j=CT)[:, :, :, j, :])
                last.then_inc(s["xd_dve"], 1)
                dve.wait_ge(s["cb_mm"], b + 1)
                dve.tensor_tensor(cb[:, :, :], bank[3][:, :].rearrange("p (c l) -> p c l", c=NC),
                                  until_row[:, :].rearrange("p (o l) -> p o l", o=1).to_broadcast([P, NC, CH]),
                                  ALU.mult).then_inc(s["cb_done"], 1)
                dve.wait_ge(s["dec_done"], b * 3 + 1)
                dve.tensor_tensor(x_dec[:, :, :].rearrange("p t (h c) -> p (t h) c", c=HP),
                                  x_dt[:, :, :].rearrange("p t (h c) -> p (t h) c", c=HP),
                                  e_end[:, :, :].rearrange("p t (h o) -> p (t h) o", o=1).to_broadcast([P, QT * NH, HP]),
                                  ALU.mult).then_inc(s["xdec_done"], 1)
                if more or ph < LAST:
                    ln_stats_vector(dve, n + 1, nxt)
                dve.wait_ge(s["cb_done"], b + 1)
                for t in range(QT):
                    dve.wait_ge(s["diff_exp"], b * 8 + 2 * t + 2)
                    for c in range(CT):
                        last = dve.tensor_tensor(decay[:, t, c, :, :], decay[:, t, c, :, :],
                                                 cb[:, t * CT + c:t * CT + c + 1, :].to_broadcast([P, SG, CH]), ALU.mult)
                    last.then_inc(s["mix_done"], 1)
                if more or ph < LAST:
                    ln_norm_vector(dve, n + 1, nxt)
                for ch in range(NC - 1):
                    t, c = divmod(ch, CT)
                    k = b * (NC - 1) + ch
                    if ch:
                        dve.wait_ge(s["st_add"], k)
                        if ch == 1:
                            dve.wait_ge(s["dec_done"], b * 3 + 3)
                        dve.tensor_tensor(s_dec[:, :].rearrange("p (h c) -> p h c", c=HP),
                                          state[:, ch, :].rearrange("p (h c) -> p h c", c=HP),
                                          e_tot[:, c, t, :].rearrange("p (h o) -> p h o", o=1).to_broadcast([P, NH, HP]),
                                          ALU.mult).then_inc(s["st_mul"], 1)
                        dve.wait_ge(s["st_mul"], b * (NC - 2) + ch)
                        dve.wait_ge(s["st_mm"], k + 1)
                        dve.tensor_tensor(state[:, ch + 1, :], bank[4 + ch % 2][:, 0:DI], s_dec[:, :],
                                          ALU.add).then_inc(s["st_add"], 1)
                    else:
                        dve.wait_ge(s["st_mm"], k + 1)
                        if not static0:
                            dve.wait_ge(s["yo_mm"], b)
                        dve.memset(state[:, 0, :], 0.0)
                        dve.tensor_copy(state[:, 1, :], bank[4][:, 0:DI]).then_inc(s["st_add"], 1)
                if more or ph < LAST:
                    ln_lo_vector(dve, n + 1, 1 - par)
                dve.wait_ge(s["yo_mm"], b + 1)
                if not static0:
                    dve.wait_ge(s["yt_mm"], b)
                for i in range(QT // 2):
                    dve.tensor_tensor(
                        y[:, 2 * i:2 * i + 2, :].rearrange("p t (h c) -> p (t h) c", c=HP),
                        bank[i][:, :].rearrange("p (h c) -> p h c", c=HP),
                        e_cum[:, 2 * i:2 * i + 2, :].rearrange("p t (h o) -> p (t h) o", o=1).to_broadcast([P, 2 * NH, HP]),
                        ALU.mult).then_inc(s["yo_mul"], 1)
                dve.wait_ge(s["yd_mm"], b + 1)
                for i in range(QT // 2):
                    dve.wait_ge(s["yo_mul"], b * 2 + i + 1)
                    dve.tensor_tensor(y[:, 2 * i:2 * i + 2, :].rearrange("p t x -> p (t x)"), bank[2 + i][:, :],
                                      y[:, 2 * i:2 * i + 2, :].rearrange("p t x -> p (t x)"),
                                      ALU.add).then_inc(s["y_sum"], 1)
                dve.wait_ge(s["y_sum"], b * 2 + 2)
                for t in range(QT):
                    dve.bn_stats(y_stats[:, t, :], y[:, t, :])
                dve.drain()
                for t in range(QT):
                    last = dve.bn_aggr(y_mv[:, t, :], y_stats[:, t, :])
                last.then_inc(s["y_mvd"], 1)
                dve.wait_ge(s["y_mvd"], b + 1)
                dve.tensor_scalar(y_var[:, :], y_mv[:, :, 1], LN_EPS, None, ALU.add).then_inc(s["y_eps"], 1)
                dve.wait_ge(s["y_pow"], b + 1)
                for t in range(QT):
                    last = dve.tensor_scalar(y[:, t, :], y[:, t, :], y_mv[:, t, 0:1], y_rstd[:, t:t + 1], ALU.subtract,
                                             ALU.mult)
                last.then_inc(s["y_nrm"], 1)
                dve.wait_ge(s["y_nrm"], b + 1)
                dve.tensor_tensor(y[:, :, :], y[:, :, :],
                                  y_w[:, :].rearrange("p (o x) -> p o x", o=1).to_broadcast([P, QT, DI]),
                                  ALU.mult).then_inc(s["y_wmul"], 1)
                dve.wait_ge(s["y_wmul"], b + 1)
                dve.tensor_tensor(y[:, :, :], y[:, :, :], z_s[:, :, :], ALU.mult).then_inc(s["y_zmul"], 1)
                dve.wait_ge(s["so_mm"], b + 1)
                xv = x_sb[:, bass.ds(b * QT, QT), :]
                dve.tensor_tensor(xv, bank[6][:, :].rearrange("p (t d) -> p t d", t=QT), xv,
                                  ALU.add).then_inc(s["x_done"], 1)
            with_pairs(dve, batch)

        DT_STEPS = 7 + len(ATANH) - 1 + 2

        def ssm_scalar(act, ph):
            act.wait_ge(s["m_loaded"], 16 * N_M)
            act.activation(wx_h[:, :], wx_st[:, :], ACT.Copy)
            act.activation(neg_a[:, :], neg_a[:, :], ACT.Exp)
            act.activation(wz_h[:, :], wz_st[:, :], ACT.Copy).then_inc(s["m_hi"], 1)

            def batch(b, par, nxt, more):
                static0 = isinstance(b, int) and b == 0
                n = ph * SEQS + b
                for t in range(QT):
                    act.wait_ge(s["zdt_mm"], b * QT + t + 1)
                    if t == 0 and not static0:
                        act.wait_ge(s["y_zmul"], b)
                    act.activation(z_s[:, t, :], bank[4 + t % 2][:, 0:DI], ACT.Silu).then_inc(s["z_done"], 1)
                for q in range(XB):
                    act.wait_ge(s["conv_step"], (b * XB + q + 1) * TAPS)
                    act.activation(x_t[:, q, :], x_t[:, q, :], ACT.Silu).then_inc(s["act_x"], 1)
                act.wait_ge(s["dt_step"], b * DT_STEPS + 2)
                act.activation(dt_e[:, :, :], dt_s[:, :, :], ACT.Exp, scale=-1.0).then_inc(s["dt_exp"], 1)
                act.wait_ge(s["bturn_mm"], b + 1)
                act.activation(b_tok[:, :, :], bank[2][:, :].rearrange("p (t n) -> p t n", t=QT),
                               ACT.Copy).then_inc(s["b_done"], 1)
                act.wait_ge(s["dec_mm"], b + 1)
                act.activation(flat_t(e_end), bank[4][:, 0:QT * NH], ACT.Exp).then_inc(s["dec_done"], 1)
                act.activation(flat_t(e_cum), bank[4][:, QT * NH:2 * QT * NH], ACT.Exp).then_inc(s["dec_done"], 1)
                act.activation(e_tot[:, :, :, :].rearrange("p c t h -> p (c t h)"), bank[5][:, :],
                               ACT.Exp).then_inc(s["dec_done"], 1)
                dec = decay[:, :, :, :, :].rearrange("p t c g l -> p (t c g l)")
                for i in range(8):
                    act.wait_ge(s["diff_mm"], b * 8 + i + 1)
                    act.activation(dec[:, i * 512:(i + 1) * 512], bank[i % 2][:, :], ACT.Exp).then_inc(s["diff_exp"], 1)
                act.wait_ge(s["xdt_done"], b + 1)
                for c in range(CT // 2):
                    for j in range(CT):
                        last = act.activation(
                            x_diag[j * CH:(j + 1) * CH, :, c, :, j * HP:(j + 1) * HP],
                            x_dt[c * CH:(c + 1) * CH, :, :].rearrange("p t (g j x) -> p t g j x", g=SG, j=CT)[:, :, :, j, :],
                            ACT.Copy)
                last.then_inc(s["xd_act"], 1)
                if more or ph < LAST:
                    ln_hi_scalar(act, n + 1, 1 - par)
                for q in range(DI // P):
                    act.wait_ge(s["yt_mm"], b + 1)
                    act.activation(y_ch[:, q, :], bank[4 + q][:, :], ACT.Copy).then_inc(s["yt_done"], 1)
            act.wait_ge(s["m_zeroed"], 1)
            with_pairs(act, batch)

        def ssm_gpsimd(pool, ph):
            pool.wait_ge(s["x_done"], SEQS)
            pool.memset(blocks[:, :], 0.0)
            pool.memset(in_chunk[:, :, :], 0.0).then_inc(s["m_ones"], 1)
            pool.wait_ge(s["m_ones"], 1)
            for c in range(CT):
                rows = slice(c * CH, (c + 1) * CH)
                pool.memset(in_chunk[rows, c, :], 1.0)
                last = pool.memset(blocks[rows, rows], 1.0)
            last.then_inc(s["m_ones"], 1)
            pool.wait_ge(s["m_ones"], 2)
            pool.affine_select(out=later[:, :], in_=blocks[:, :], compare_op=ALU.is_gt, fill=0.0, base=0,
                               pattern=[[-1, P]], channel_multiplier=1)
            pool.affine_select(out=until[:, :], in_=blocks[:, :], compare_op=ALU.is_ge, fill=0.0, base=0,
                               pattern=[[1, P]], channel_multiplier=-1).then_inc(s["m_tri"], 1)
            pool.wait_ge(s["m_tri"], 1)
            for c in range(CT):
                rows = slice(c * CH, (c + 1) * CH)
                last = pool.tensor_copy(until_row[rows, :], until[rows, rows])
            last.then_inc(s["m_const"], 1)

            def batch(b, par, nxt, more):
                if more or ph < LAST:
                    ln_rstd_gpsimd(pool, ph * SEQS + b + 1)
                pool.wait_ge(s["y_eps"], b + 1)
                pool.tensor_tensor(y_rstd[:, :], y_var[:, :], half_neg[:, :], ALU.pow).then_inc(s["y_pow"], 1)
            with_pairs(pool, batch)

        N_M = 9

        def ssm_sync(sp, ph):
            if ph:
                sp.wait_ge(s["x_done"], SEQS)
            for dst, src in (
                (wx_st[:, :], w["in_wT"][:, DI:DI + XB * P]),
                (wz_st[:, 0:DI], w["in_wT"][:, 0:DI]),
                (wz_st[:, DI:DI + NH], w["in_wT"][:, DI + XB * P:DI + XB * P + NH]),
                (w_out[:, :, :], w["out_wT"].rearrange("(q p) d -> p q d", p=P)),
                (conv_w[:, :, :], w["conv_w"].rearrange("(q p) k -> p q k", p=P)),
                (conv_b[:, :], w["conv_b"]),
                (dt_bias[:, :], w["dt_bias"].rearrange("(o h) -> o h", o=1).to_broadcast([P, NH])),
                (neg_a[:, :], w["A_log"].rearrange("(o h) -> o h", o=1).to_broadcast([P, NH])),
                (y_w[:, :], w["ln_w"].rearrange("(o x) -> o x", o=1).to_broadcast([P, DI])),
            ):
                sp.dma_start(dst, src).then_inc(s["m_loaded"], 16)

        def flat3(t):
            return t[:, :, :].rearrange("p e f -> p (e f)")

        def flat4(t):
            return t[:, :, :, :].rearrange("p e c d -> p (e c d)")

        W_SPLITS = [[flat3(t) for t in (wg_st, wg_h, wg_l)], [flat3(t) for t in (wu_st, wu_h, wu_l)],
                    [flat4(t) for t in (wd_st, wd_h, wd_l)], [t[:, :] for t in (wr_st, wr_h, wr_l)]]

        @block.sync
        def _(sp):
            sp.dma_start(x_sb[:, 0:QT, :], x_in[0].rearrange("(t p) d -> p t d", p=P)).then_inc(s["x0_loaded"], 16)
            n_w = 0
            for dst, src in (
                (wqT_st[:, :, :], w["WqT"].rearrange("h k d -> k h d")),
                (wkT_st[:, :, :], w["WkT"].rearrange("h k c -> k h c")),
                (wkv_st[:, :], w["Wkv_down"]),
                (wvT_st[:, :, :], w["WvT"].rearrange("h k c -> k h c")),
                (wo_st[:, :, :], w["Wout"].rearrange("h k d -> k h d")),
                (wr_st[:, :], w["Wr"]),
                (wg_st[:, 0, :], w["Sg"]), (wg_st[:, 1:XP, :], w["Wg"].rearrange("e h f -> h e f")),
                (wu_st[:, 0, :], w["Su"]), (wu_st[:, 1:XP, :], w["Wu"].rearrange("e h f -> h e f")),
                (wd_st[:, 0, :, :], w["Sd"].rearrange("(c p) d -> p c d", p=P)),
                (wd_st[:, 1:XP, :, :].rearrange("p e c d -> p (e c) d"),
                 w["Wd"].rearrange("e (c p) d -> p (e c) d", p=P)),
            ):
                sp.dma_start(dst, src).then_inc(s["w_loaded"], 16)
                n_w += 1
            assert n_w == N_W
            for q in range(1, SEQS):
                sp.dma_start(x_sb[:, q * QT:(q + 1) * QT, :],
                             x_in[q].rearrange("(t p) d -> p t d", p=P)).then_inc(s["x_loaded"], 16)
            if "attn" in phases:
                attn_sync(sp)
            if "ssm" in phases:
                ssm_sync(sp, phases.index("ssm"))
            with sp.Fori(0, SEQS) as b:
                sp.wait_ge(s["x_done"], LAST * SEQS + 1 + b)
                sp.dma_start(out[bass.ds(b, 1), :, :].rearrange("o (t p) d -> p (o t) d", p=P),
                             x_sb[:, bass.ds(b * QT, QT), :]).then_inc(s["stored"], 16)
            sp.wait_ge(s["stored"], 16 * SEQS)

        @block.gpsimd
        def _(pool):
            pool.memset(ident[:, :], 0.0)
            pool.memset(causal[:, :], 0.0)
            pool.memset(tie[:, :, :], 1.0)
            pool.memset(half_neg[:, :], -0.5).then_inc(s["c_zero"], 1)
            pool.wait_ge(s["c_zero"], 1)
            pool.affine_select(out=ident[:, :], in_=ident[:, :], compare_op=ALU.not_equal, fill=1.0, base=0,
                               pattern=[[-1, P]], channel_multiplier=1)
            pool.affine_select(out=causal[:, :], in_=causal[:, :], compare_op=ALU.is_ge, fill=MASKED, base=0,
                               pattern=[[-1, P]], channel_multiplier=1)
            pool.affine_select(out=tie[:, :, :], in_=tie[:, :, :], compare_op=ALU.is_gt, fill=0.0, base=0,
                               pattern=[[1, E], [-1, E]], channel_multiplier=0).then_inc(s["c_made"], 1)
            ln_rstd_gpsimd(pool, 0)
            for ph, name in enumerate(phases):
                if name == "attn":
                    attn_gpsimd(pool)
                elif name == "ssm":
                    ssm_gpsimd(pool, ph)
                else:
                    ffn_gpsimd(pool, FN[ph], ph)

        @block.tensor
        def _(pe):
            pe.sem_inc(s["xt_free"], 1)
            pe.wait_ge(s["w_loaded"], 16 * N_W)
            for h in range(H):
                pe.matmul(bank[0][:, h * LD:(h + 1) * LD], wqT_st[:, h, :], wkT_st[:, h, :], start=True, stop=True)
            for h in range(H):
                g, j = divmod(h, HG)
                last = pe.matmul(bank[1][j * LD:(j + 1) * LD, g * D:(g + 1) * D], wvT_st[:, h, :], wo_st[:, h, :],
                                 start=True, stop=True)
            last.then_inc(s["wfold_mm"], 1)
            pe.wait_ge(s["c_made"], 1)
            ln_turn_tensor(pe, 0, first=True)
            pe.wait_ge(s["c_round"], 1)
            pe.wait_ge(s["wfold_done"], 1)
            for ph, name in enumerate(phases):
                if name == "attn":
                    attn_tensor(pe)
                elif name == "ssm":
                    ssm_tensor(pe, ph)
                else:
                    ffn_tensor(pe, FN[ph], ph)

        @block.scalar
        def _(act):
            act.wait_ge(s["w_loaded"], 16 * N_W)
            for st, hi, lo in W_SPLITS:
                act.activation(hi, st, ACT.Copy)
            for r in range(HG):
                last = act.activation(wkv_h[:, r, :], wkv_st[:, :], ACT.Copy)
            last.then_inc(s["w_hi"], 1)
            act.wait_ge(s["wfold_mm"], 1)
            act.activation(wq_h[:, :], bank[0][:, :], ACT.Copy, scale=HD ** -0.5).then_inc(s["wfold_hi"], 1)
            ln_hi_scalar(act, 0, 0, first=True)
            for ph, name in enumerate(phases):
                if name == "attn":
                    attn_scalar(act)
                elif name == "ssm":
                    ssm_scalar(act, ph)
                else:
                    ffn_scalar(act, FN[ph], ph)

        @block.vector
        def _(dve):
            dve.wait_ge(s["x0_loaded"], 16)
            ln_stats_vector(dve, 0, 0)
            dve.wait_ge(s["c_made"], 1)
            dve.tensor_copy(ident_r[:, :], ident[:, :])
            dve.tensor_copy(causal_r[:, :], causal[:, :]).then_inc(s["c_round"], 1)
            ln_norm_vector(dve, 0, 0, first=True)
            dve.wait_ge(s["w_hi"], 1)
            for st, hi, lo in W_SPLITS:
                dve.tensor_tensor(lo, st, hi, ALU.subtract)
            for r in range(HG):
                dve.tensor_tensor(wkv_l[:, r, :], wkv_st[:, :], wkv_h[:, r, :], ALU.subtract)
            dve.wait_ge(s["wfold_hi"], 1)
            dve.scalar_tensor_tensor(out=wq_l[:, :], in0=bank[0][:, :], scalar=HD ** -0.5, in1=wq_h[:, :],
                                     op0=ALU.mult, op1=ALU.subtract)
            dve.tensor_copy(wvo[:, :, :], bank[1][:, :].rearrange("p (g d) -> p g d", g=G)).then_inc(s["wfold_done"], 1)
            ln_lo_vector(dve, 0, 0)
            dve.wait_ge(s["x_loaded"], 16 * (SEQS - 1))
            for ph, name in enumerate(phases):
                if name == "attn":
                    attn_vector(dve)
                elif name == "ssm":
                    ssm_vector(dve, ph)
                else:
                    ffn_vector(dve, FN[ph], ph)


PHASES = ("attn", "ffn", "ssm", "ffn")


def kernel(**inputs):
    import numpy as np
    import concourse.bacc as bacc
    from concourse.bass_utils import run_bass_kernel_spmd as run

    a = {k: np.asarray(v) for k, v in inputs.items()}
    arrays = {
        "x": a["L0_attn_a_x_bld"],
        "WqT": a["L0_attn_a_Wq"].transpose(1, 2, 0),
        "Wkv_down": a["L0_attn_a_Wkv_down"],
        "WkT": a["L0_attn_a_Wk_up"].transpose(1, 2, 0),
        "WvT": a["L0_attn_a_Wv_up"].transpose(1, 2, 0),
        "Wout": a["L0_attn_a_Wout"],
        "Wr": a["L0_ffn_Wr"], "Wg": a["L0_ffn_Wg"], "Wu": a["L0_ffn_Wu"], "Wd": a["L0_ffn_Wd"],
        "in_wT": a["L0_attn_b_in_proj_w"].T, "out_wT": a["L0_attn_b_out_proj_w"].T,
        "conv_w": a["L0_attn_b_conv_w"], "conv_b": a["L0_attn_b_conv_b"].reshape(XB, P).T, "dt_bias": a["L0_attn_b_dt_bias"],
        "A_log": a["L0_attn_b_A_log"], "ln_w": a["L0_attn_b_ln_w"],
        "Sg": a["L0_ffn_Sg"], "Su": a["L0_ffn_Su"], "Sd": a["L0_ffn_Sd"],
    }
    arrays = {k: np.ascontiguousarray(v) for k, v in arrays.items()}
    nc = bacc.Bacc("TRN2", target_bir_lowering=False, num_devices=1)
    w = {k: nc.dram_tensor(f"in_{k}", v.shape, F32, kind="ExternalInput").ap() for k, v in arrays.items()}
    out = nc.dram_tensor("out", arrays["x"].shape, F32, kind="ExternalOutput").ap()
    program(nc, w["x"], out, w, PHASES)
    r = run(nc, [{f"in_{k}": v for k, v in arrays.items()}], core_ids=[0])
    return r.results[0]["out"]
```

```python
from contextlib import ExitStack

import concourse.bass as bass
from concourse import mybir

F32 = mybir.dt.float32
F32R = mybir.dt.float32r
ALU = mybir.AluOpType
ACT = mybir.ActivationFunctionType
AX = mybir.AxisListType

P = 128
SEQS = 16
L = 512
QT = L // P
PAIRS = SEQS // 2
D = 128
LN_EPS = 1e-5
H, HD, LD = 16, 64, 32
HG = P // LD
G = H // HG
UNITS = 3
UPS = UNITS * H
MASKED = -1.0e30
E, F, TOPK = 8, 256, 2
FC = F // P
XP = E + 1
MU = XP * FC
ROUTE_EPS = 1e-20

DI, NS, NH, HP = 256, 128, 32, 8
TAPS, CH = 4, 32
CT = P // CH
NC = L // CH
XB = (DI + 2 * NS) // P
SG = NH // CT
ATANH = [1.0 / n for n in range(17, 1, -2)]

UNIT_TILES = [[(3, 0)], [(2, 0), (0, 384)], [(1, 0)]]
UNIT_COLS = [512, 512, 256]
UNIT_AT = [0, 512, 1024]
HEAD_COLS = 1280


def program(nc, x_in, out, w, phases):
    ctx = ExitStack()
    with ctx:
        stack = ctx

        def sb(name, shape, dt=F32):
            return stack.enter_context(nc.sbuf_tensor(name, shape, dt))

        def sem(name):
            return ctx.enter_context(nc.semaphore(name))

        bank = [ctx.enter_context(nc.psum_tensor(f"bank{i}", [P, 512], F32)) for i in range(8)]
        ln_bank = bank[7]

        x_sb = sb("x_sb", [P, SEQS * QT, D])
        ident = sb("ident", [P, P])
        ident_r = sb("ident_r", [P, P], F32R)
        causal = sb("causal", [P, P])
        causal_r = sb("causal_r", [P, P], F32R)
        half_neg = sb("half_neg", [P, QT])
        stats = sb("stats", [P, QT, 6])
        mv = sb("mv", [P, QT, 2])
        var_eps = sb("var_eps", [P, QT])
        rstd = sb("rstd", [P, QT])
        xn = sb("xn", [P, QT, D])
        xh = [sb(f"xh{i}", [P, L], F32R) for i in range(2)]
        xl = [sb(f"xl{i}", [P, L], F32R) for i in range(2)]
        wq_h = sb("wq_h", [P, G * P], F32R)
        wq_l = sb("wq_l", [P, G * P], F32R)
        wkv_h = sb("wkv_h", [P, HG, LD], F32R)
        wkv_l = sb("wkv_l", [P, HG, LD], F32R)
        wvo = sb("wvo", [P, G, D])
        wg_h = sb("wg_h", [P, XP, F], F32R)
        wg_l = sb("wg_l", [P, XP, F], F32R)
        wu_h = sb("wu_h", [P, XP, F], F32R)
        wu_l = sb("wu_l", [P, XP, F], F32R)
        wd_h = sb("wd_h", [P, XP, FC, D], F32R)
        wd_l = sb("wd_l", [P, XP, FC, D], F32R)
        wr_h = sb("wr_h", [P, E], F32R)
        wr_l = sb("wr_l", [P, E], F32R)
        tie = sb("tie", [P, E, E])
        stack = ExitStack()
        wg_st = sb("wg_st", [P, XP, F])
        wu_st = sb("wu_st", [P, XP, F])
        wd_st = sb("wd_st", [P, XP, FC, D])
        wr_st = sb("wr_st", [P, E])
        wkv_st = sb("wkv_st", [P, LD])
        wqT_st = sb("wqT_st", [HD, H, D])
        wkT_st = sb("wkT_st", [HD, H, LD])
        wvT_st = sb("wvT_st", [HD, H, LD])
        wo_st = sb("wo_st", [HD, H, D])
        stack.close()
        stack = ExitStack()
        q_h = sb("q_h", [P, L], F32R)
        q_l = sb("q_l", [P, L], F32R)
        qs = sb("qs", [P, H, L], F32R)
        lat_hi = sb("lat_hi", [P, L], F32R)
        ls = [sb(f"ls{i}", [P, L], F32R) for i in range(2)]
        lat_tok = [sb(f"lat_tok{i}", [P, QT, LD]) for i in range(2)]
        neg_max = sb("neg_max", [P, 2, H, QT])
        row_sum = sb("row_sum", [P, 2, H, QT])
        r_inv = sb("r_inv", [P, HG, QT])
        probs = sb("probs", [P, 3, 512])
        probs_t = sb("probs_t", [P, 2, HG, HEAD_COLS])
        y_t = sb("y_t", [P, L])
        y_q = sb("y_q", [P, QT, HG, LD])
        y_n = sb("y_n", [P, G, L])
        stack.close()
        SLOTS = 3
        stack = ExitStack()
        silu_g = sb("silu_g", [P, 2, L])
        hid = sb("hid", [P, SLOTS, L])
        y_exp = sb("y_exp", [P, 2, L])
        hid_h = [sb(f"hid_h{i}", [P, L], F32R) for i in range(SLOTS)]
        hid_l = [sb(f"hid_l{i}", [P, L], F32R) for i in range(SLOTS)]
        r_max = sb("r_max", [P, QT])
        r_log = sb("r_log", [P, QT, E])
        r_exp = sb("r_exp", [P, QT, E])
        r_sum = sb("r_sum", [P, QT])
        r_one = sb("r_one", [P, QT])
        score = sb("score", [P, QT, E])
        above = sb("above", [P, QT, E, E])
        equal = sb("equal", [P, QT, E, E])
        rank = sb("rank", [P, QT, E])
        gate = sb("gate", [P, 2, QT, E])
        stack.close()

        stack = ExitStack()
        x_diag = sb("x_diag", [P, QT, CT, SG, CT * HP])
        x_t = sb("x_t", [P, XB, L])
        w_stack = stack
        z_s = sb("z_s", [P, QT, DI])
        stack = ExitStack()
        a_cum = sb("a_cum", [P, NC * SG, CH])
        stack.close()
        stack = w_stack
        state = sb("state", [P, NC, DI])
        stack = ExitStack()
        wx_st = sb("wx_st", [P, XB * P])
        wz_st = sb("wz_st", [P, DI + NH])
        stack.close()
        stack = w_stack
        decay = sb("decay", [P, QT, CT, SG, CH])
        wx_h = sb("wx_h", [P, XB * P], F32R)
        wx_l = sb("wx_l", [P, XB * P], F32R)
        wz_h = sb("wz_h", [P, DI + NH], F32R)
        wz_l = sb("wz_l", [P, DI + NH], F32R)
        w_out = sb("w_out", [P, DI // P, D])
        conv_w = sb("conv_w", [P, XB, TAPS])
        conv_b = sb("conv_b", [P, XB])
        dt_bias = sb("dt_bias", [P, NH])
        neg_a = sb("neg_a", [P, NH])
        y_w = sb("y_w", [P, DI])
        dt_v = sb("dt_v", [P, QT, NH])
        dt_e = sb("dt_e", [P, QT, NH])
        dt_r = sb("dt_r", [P, QT, NH])
        dt_q = sb("dt_q", [P, QT, NH])
        dt_s = sb("dt_s", [P, QT, NH])
        dt_p = sb("dt_p", [P, QT, NH])
        dt = sb("dt", [P, QT, NH])
        a_tok = sb("a_tok", [P, QT, NH])
        a_row = sb("a_row", [P, QT, CT, SG])
        cb = sb("cb", [P, NC, CH])
        b_tok = sb("b_tok", [P, QT, NS])
        x_dt = sb("x_dt", [P, QT, DI])
        x_dec = sb("x_dec", [P, QT, DI])
        e_end = sb("e_end", [P, QT, NH])
        e_cum = sb("e_cum", [P, QT, NH])
        e_tot = sb("e_tot", [P, CT, QT, NH])
        s_dec = sb("s_dec", [P, DI])
        y = sb("y", [P, QT, DI])
        y_stats = sb("y_stats", [P, QT, 6])
        y_mv = sb("y_mv", [P, QT, 2])
        y_var = sb("y_var", [P, QT])
        y_rstd = sb("y_rstd", [P, QT])
        y_ch = sb("y_ch", [P, DI // P, L])
        blocks = sb("blocks", [P, P])
        later = sb("later", [P, P])
        until = sb("until", [P, P])
        until_row = sb("until_row", [P, CH])
        in_chunk = sb("in_chunk", [P, CT, P])
        stack.close()

        s = {n: sem(n) for n in (
            "x0_loaded x_loaded w_loaded c_zero c_made c_round w_hi wfold_mm wfold_hi wfold_done "
            "ln_var ln_eps ln_rstd ln_xn ln_t ln_hi ln_lo xt_free x_done "
            "q_mm q_hi q_lo q_dma s_mm s_max s_exp p_t pt_act pt_dve pv_mm y_ev y_back y_rinv y_norm y_fwd y_ev2 "
            "o_mm stored "
            "m_loaded m_const m_ones m_tri m_hi m_split m_nega m_zeroed xbc_mm conv_step conv_done act_x zdt_mm z_done dt_read dt_step "
            "dt_exp a_done a_rows cum_done xturn_mm xdt_done dec_mm dec_done xdec_done bturn_mm b_done cb_mm cb_done "
            "diff_mm diff_exp mix_done xd_act xd_dve st_mm st_mul st_add yd_mm yo_mm yo_mul y_sum y_mvd y_eps y_pow y_nrm "
            "y_wmul y_zmul yt_mm yt_done so_mm").split()}
        fs = [{n: sem(f"{n}_{f}") for n in (
            "log_mm r_step r_exped gate_mm up_mm silu_done hid_done hid_hi hid_lo down_used down_mm acc_done").split()}
            for f in range(2)]
        block = ctx.enter_context(nc.Block())

        def mm3(pe, o, a_h, a_l, b_h, b_l):
            pe.matmul(o, a_h, b_h, start=True, stop=False)
            pe.matmul(o, a_l, b_h, start=False, stop=False)
            return pe.matmul(o, a_h, b_l, start=False, stop=True)

        LAST = len(phases) - 1
        FN = {ph: sum(p == "ffn" for p in phases[:ph]) for ph in range(len(phases))}
        N_W = 12

        def ln_stats_vector(dve, n, b):
            for t in range(QT):
                dve.bn_stats(stats[:, t, :], x_sb[:, bass.ds(b * QT + t, 1), :].rearrange("p o d -> p (o d)"))
            dve.drain()
            for t in range(QT):
                last = dve.bn_aggr(mv[:, t, :], stats[:, t, :])
            last.then_inc(s["ln_var"], 1)
            dve.wait_ge(s["ln_var"], n + 1)
            dve.tensor_scalar(var_eps[:, :], mv[:, :, 1], LN_EPS, None, ALU.add).then_inc(s["ln_eps"], 1)

        def ln_rstd_gpsimd(pool, n):
            pool.wait_ge(s["ln_eps"], n + 1)
            pool.tensor_tensor(rstd[:, :], var_eps[:, :], half_neg[:, :], ALU.pow).then_inc(s["ln_rstd"], 1)

        def ln_norm_vector(dve, n, b, first=False):
            dve.wait_ge(s["ln_rstd"], n + 1)
            if not first:
                dve.wait_ge(s["ln_t"], n)
            for t in range(QT):
                last = dve.tensor_scalar(xn[:, t, :],
                                         x_sb[:, bass.ds(b * QT + t, 1), :].rearrange("p o d -> p (o d)"),
                                         mv[:, t, 0:1], rstd[:, t:t + 1], ALU.subtract, ALU.mult)
            last.then_inc(s["ln_xn"], 1)

        def ln_turn_tensor(pe, n, first=False):
            pe.wait_ge(s["ln_xn"], n + 1)
            if not first:
                pe.wait_ge(s["ln_lo"], n)
            for t in range(QT):
                last = pe.transpose(ln_bank[:, t * P:(t + 1) * P], xn[:, t, :], ident[:, :])
            last.then_inc(s["ln_t"], 1)

        def ln_hi_scalar(act, n, par, first=False):
            act.wait_ge(s["ln_t"], n + 1)
            if not first:
                act.wait_ge(s["xt_free"], n)
            act.activation(xh[par][:, :], ln_bank[:, :], ACT.Copy).then_inc(s["ln_hi"], 1)

        def ln_lo_vector(dve, n, par):
            dve.wait_ge(s["ln_hi"], n + 1)
            dve.tensor_tensor(xl[par][:, :], ln_bank[:, :], xh[par][:, :], ALU.subtract).then_inc(s["ln_lo"], 1)

        Q_DMAS = 3 * HG
        A_ITEMS = 2 + G

        def proj_tensor(pe, b, par, item, first=False):
            if item == 0:
                pe.wait_ge(s["ln_lo"], b + 1)
            elif item > 0:
                pe.wait_ge(s["q_lo"], b * A_ITEMS + item)
            if item == 0:
                last = mm3(pe, ln_bank[0:3 * LD, :], wkv_h[:, 0:3, :].rearrange("p r c -> p (r c)"),
                           wkv_l[:, 0:3, :].rearrange("p r c -> p (r c)"), xh[par][:, :], xl[par][:, :])
            elif item == 1:
                for t in range(QT):
                    c = slice(t * P, (t + 1) * P)
                    last = mm3(pe, ln_bank[:, t * LD:(t + 1) * LD], xh[par][:, c], xl[par][:, c],
                               wkv_h[:, 0, :], wkv_l[:, 0, :])
            else:
                c = slice((item - 2) * P, (item - 1) * P)
                last = mm3(pe, ln_bank[:, :], wq_h[:, c], wq_l[:, c], xh[par][:, :], xl[par][:, :])
            last.then_inc(s["q_mm"], 1)

        def proj_scalar(act, b, par, item):
            act.wait_ge(s["q_mm"], b * A_ITEMS + item + 1)
            if item == 0:
                act.activation(ls[par][0:64, :], ln_bank[0:64, :], ACT.Copy)
                act.activation(lat_hi[64:96, :], ln_bank[64:96, :], ACT.Copy).then_inc(s["q_hi"], 1)
            elif item == 1:
                act.activation(lat_tok[par][:, :, :], ln_bank[:, 0:QT * LD].rearrange("p (t c) -> p t c", t=QT),
                               ACT.Copy).then_inc(s["q_hi"], 1)
            else:
                g = item - 2
                if not (isinstance(b, int) and b == 0 and g == 0):
                    act.wait_ge(s["q_dma"], (b * G + g) * 16 * Q_DMAS)
                act.activation(q_h[:, :], ln_bank[:, :], ACT.Copy).then_inc(s["q_hi"], 1)

        def proj_vector(dve, b, par, item):
            dve.wait_ge(s["q_hi"], b * A_ITEMS + item + 1)
            if item == 0:
                dve.tensor_tensor(ls[par][64:96, :], ln_bank[64:96, :], lat_hi[64:96, :],
                                  ALU.subtract).then_inc(s["q_lo"], 1)
            elif item == 1:
                dve.sem_inc(s["q_lo"], 1)
            else:
                g = item - 2
                dve.tensor_tensor(q_l[:, :], ln_bank[:, :], q_h[:, :], ALU.subtract).then_inc(s["q_lo"], 1)

        def proj_sync(sp, b, g, first=False):
            parts, used = b * A_ITEMS + 2 + g + 1, (b - 1) * UPS + (g + 1) * HG * UNITS
            if not isinstance(b, int):
                parts, used = sp.to_reg(parts), sp.to_reg(used)
            sp.wait_ge(s["q_lo"], parts)
            if not first:
                sp.wait_ge(s["s_mm"], used)
            for j in range(HG):
                for r, part in enumerate((q_h, q_l, q_h)):
                    sp.dma_start(qs[r * LD:(r + 1) * LD, g * HG + j, :].bitcast(F32),
                                 part[j * LD:(j + 1) * LD, :].bitcast(F32)).then_inc(s["q_dma"], 16)

        def scores_tensor(pe, b, par, u):
            h, k = divmod(u, UNITS)
            g = h // HG
            o = bank[u % 3]
            if u % (HG * UNITS) == 0:
                pe.wait_ge(s["q_dma"], (b * G + g + 1) * 16 * Q_DMAS)
            if not (isinstance(b, int) and b == 0 and u < 3):
                pe.wait_ge(s["s_exp"], b * UPS + u - 2)
            for qt, at in UNIT_TILES[k]:
                n = (qt + 1) * P
                q = qs[0:3 * LD, h, qt * P:(qt + 1) * P]
                pe.matmul(o[:, at:at + n], q, ls[par][0:3 * LD, 0:n], start=(at == 0), stop=False, skip_group_check=True)
                last = pe.matmul(o[:, at + qt * P:at + n], ident_r[:, :], causal_r[:, :], start=False, stop=True,
                                 skip_group_check=True)
            last.then_inc(s["s_mm"], 1)

        def max_vector(dve, b, par, u):
            h, k = divmod(u, UNITS)
            dve.wait_ge(s["s_mm"], b * UPS + u + 1)
            for qt, at in UNIT_TILES[k]:
                last = dve.tensor_reduce(neg_max[:, par, h, qt:qt + 1], bank[u % 3][:, at:at + (qt + 1) * P], AX.X,
                                         ALU.max, negate=True)
            last.then_inc(s["s_max"], 1)

        def exp_scalar(act, b, par, u):
            h, k = divmod(u, UNITS)
            act.wait_ge(s["s_max"], b * UPS + u + 1)
            if not (isinstance(b, int) and b == 0 and u < 3):
                act.wait_ge(s["p_t"], b * UPS + u - 2)
            for qt, at in UNIT_TILES[k]:
                c = slice(at, at + (qt + 1) * P)
                last = act.activation(probs[:, u % 3, c], bank[u % 3][:, c], ACT.Exp,
                                      bias=neg_max[:, par, h, qt:qt + 1], accum_out=row_sum[:, par, h, qt:qt + 1])
            last.then_inc(s["s_exp"], 1)

        def turn_tensor(pe, b, u):
            k = u % UNITS
            pe.wait_ge(s["s_exp"], b * UPS + u + 1)
            if not (isinstance(b, int) and b == 0 and u < 2):
                pe.wait_ge(s["pt_act" if u % 2 == 0 else "pt_dve"], b * (UPS // 2) + u // 2)
            for c in range(0, UNIT_COLS[k], P):
                last = pe.transpose(bank[3 + u % 2][:, c:c + P], probs[:, u % 3, c:c + P], ident[:, :])
            last.then_inc(s["p_t"], 1)

        def turned_copy(eng, b, u):
            h, k = divmod(u, UNITS)
            g = h // HG
            eng.wait_ge(s["p_t"], b * UPS + u + 1)
            if u % (HG * UNITS) < 2 and not (isinstance(b, int) and b == 0 and g < 2):
                eng.wait_ge(s["pv_mm"], b * G + g - 1)
            o = probs_t[:, g % 2, h % HG, UNIT_AT[k]:UNIT_AT[k] + UNIT_COLS[k]]
            i = bank[3 + u % 2][:, 0:UNIT_COLS[k]]
            return o, i

        def turned_scalar(act, b, u):
            o, i = turned_copy(act, b, u)
            act.activation(o, i, ACT.Copy).then_inc(s["pt_act"], 1)

        def turned_vector(dve, b, u):
            o, i = turned_copy(dve, b, u)
            dve.tensor_copy(o, i).then_inc(s["pt_dve"], 1)

        def values_tensor(pe, b, par, g):
            pe.wait_ge(s["pt_act"], b * (UPS // 2) + (g + 1) * HG * UNITS // 2)
            pe.wait_ge(s["pt_dve"], b * (UPS // 2) + (g + 1) * HG * UNITS // 2)
            if not (isinstance(b, int) and b == 0 and g == 0):
                pe.wait_ge(s["y_ev"], b * G + g)
                if g == 0:
                    pe.wait_ge(s["x_done"], b)
            first = [True] * HG
            for k in range(UNITS):
                for qt, at in UNIT_TILES[k]:
                    for kb in range(qt + 1):
                        for j in range(HG):
                            c = UNIT_AT[k] + at + kb * P
                            last = pe.matmul(bank[5][j * LD:(j + 1) * LD, qt * P:(qt + 1) * P], lat_tok[par][:, kb, :],
                                             probs_t[:, g % 2, j, c:c + P], start=first[j], stop=(kb == qt),
                                             skip_group_check=True)
                            if g == G - 1 and first[j] and j == 0:
                                last.then_inc(s["xt_free"], 1)
                            first[j] = False
            last.then_inc(s["pv_mm"], 1)

        def y_copy_scalar(act, b, g):
            act.wait_ge(s["pv_mm"], b * G + g + 1)
            if not (isinstance(b, int) and b == 0 and g == 0):
                act.wait_ge(s["y_back"], b * G + g)
            act.activation(y_t[:, :], bank[5][:, :], ACT.Copy).then_inc(s["y_ev"], 1)

        def y_back_tensor(pe, b, g):
            pe.wait_ge(s["y_ev"], b * G + g + 1)
            if not (isinstance(b, int) and b == 0 and g == 0):
                pe.wait_ge(s["y_ev2"], b * G + g)
            for t in range(QT):
                last = pe.transpose(bank[6][:, t * P:(t + 1) * P], y_t[:, t * P:(t + 1) * P], ident[:, :])
            last.then_inc(s["y_back"], 1)

        def y_norm_vector(dve, b, par, g):
            dve.wait_ge(s["s_exp"], b * UPS + (g + 1) * HG * UNITS)
            dve.reciprocal(r_inv[:, :, :], row_sum[:, par, g * HG:(g + 1) * HG, :]).then_inc(s["y_rinv"], 1)
            dve.wait_ge(s["y_rinv"], b * G + g + 1)
            dve.wait_ge(s["y_back"], b * G + g + 1)
            if not (isinstance(b, int) and b == 0 and g == 0):
                dve.wait_ge(s["y_fwd"], b * G + g)
            dve.tensor_tensor(y_q[:, :, :, :], bank[6][:, :].rearrange("p (t j c) -> p t j c", t=QT, j=HG),
                              r_inv[:, :, :].rearrange("p j (t o) -> p t j o", o=1).to_broadcast([P, QT, HG, LD]),
                              ALU.mult).then_inc(s["y_norm"], 1)

        def y_fwd_tensor(pe, b, g):
            pe.wait_ge(s["y_norm"], b * G + g + 1)
            for t in range(QT):
                last = pe.transpose(bank[6][:, t * P:(t + 1) * P], y_q[:, t, :, :].rearrange("p j c -> p (j c)"),
                                    ident[:, :])
            last.then_inc(s["y_fwd"], 1)

        def y_copy2_scalar(act, b, g):
            act.wait_ge(s["y_fwd"], b * G + g + 1)
            if g == 0 and not (isinstance(b, int) and b == 0):
                act.wait_ge(s["o_mm"], b)
            act.activation(y_n[:, g, :], bank[6][:, :], ACT.Copy).then_inc(s["y_ev2"], 1)

        def out_tensor(pe, b):
            pe.wait_ge(s["y_ev2"], b * G + G)
            for t in range(QT):
                for g in range(G):
                    last = pe.matmul(bank[5][:, t * P:(t + 1) * P], y_n[:, g, t * P:(t + 1) * P], wvo[:, g, :],
                                     start=(g == 0), stop=(g == G - 1))
            last.then_inc(s["o_mm"], 1)

        def out_vector(dve, b):
            dve.wait_ge(s["o_mm"], b + 1)
            xv = x_sb[:, bass.ds(b * QT, QT), :]
            dve.tensor_tensor(xv, bank[5][:, :].rearrange("p (t d) -> p t d", t=QT), xv,
                              ALU.add).then_inc(s["x_done"], 1)

        GU = HG * UNITS
        LN_AT = {"stats": 2, "norm": 5, "turn": 8, "hi": 9, "lo": 10}
        PROJ_AT = {12: 0, 15: 1, 18: 2, 28: 3, 39: 4}
        PROJ_LAST = 2

        def before(b, par):
            return b - 1, 1 - par

        def has_before(b):
            return not (isinstance(b, int) and b == 0)

        def attn_tensor(pe):
            def finish(b, par, v):
                if v == 3:
                    values_tensor(pe, b, par, G - 1)
                if v == 6:
                    y_back_tensor(pe, b, G - 1)
                if v == 9:
                    y_fwd_tensor(pe, b, G - 1)
                if v == 11:
                    out_tensor(pe, b)

            def batch(b, par, nxt, proj):
                for u in range(UPS):
                    if u + 2 < UPS:
                        scores_tensor(pe, b, par, u + 2)
                    elif proj:
                        scores_tensor(pe, b + 1, 1 - par, u + 2 - UPS)
                    if u:
                        turn_tensor(pe, b, u - 1)
                    elif has_before(b):
                        turn_tensor(pe, b - 1, UPS - 1)
                    g, v = divmod(u, GU)
                    if g == 0 and has_before(b):
                        finish(*before(b, par), v)
                    if g and v == 3:
                        values_tensor(pe, b, par, g - 1)
                    if g and v == 6:
                        y_back_tensor(pe, b, g - 1)
                    if g and v == 9:
                        y_fwd_tensor(pe, b, g - 1)
                    if u == LN_AT["turn"]:
                        ln_turn_tensor(pe, b + 1)
                    if u == PROJ_LAST:
                        proj_tensor(pe, b, par, A_ITEMS - 1)
                    if proj and u in PROJ_AT:
                        proj_tensor(pe, b + 1, 1 - par, PROJ_AT[u])

            for item in range(A_ITEMS - 1):
                proj_tensor(pe, 0, 0, item)
            scores_tensor(pe, 0, 0, 0)
            scores_tensor(pe, 0, 0, 1)
            with_pairs(pe, batch)
            turn_tensor(pe, SEQS - 1, UPS - 1)
            for v in range(GU):
                finish(SEQS - 1, 1, v)

        def attn_vector(dve):
            def finish(b, par, v):
                if v == 7:
                    y_norm_vector(dve, b, par, G - 1)
                if v == 11:
                    out_vector(dve, b)

            def batch(b, par, nxt, proj):
                for u in range(UPS):
                    max_vector(dve, b, par, u)
                    if u % 2 and u >= 2:
                        turned_vector(dve, b, u - 2)
                    elif u == 1 and has_before(b):
                        turned_vector(dve, b - 1, UPS - 1)
                    g, v = divmod(u, GU)
                    if g == 0 and has_before(b):
                        finish(*before(b, par), v)
                    if g and v == 7:
                        y_norm_vector(dve, b, par, g - 1)
                    if u == LN_AT["stats"]:
                        ln_stats_vector(dve, b + 1, nxt)
                    if u == PROJ_LAST + 1:
                        proj_vector(dve, b, par, A_ITEMS - 1)
                    if u == LN_AT["norm"]:
                        ln_norm_vector(dve, b + 1, nxt)
                    if u == LN_AT["lo"]:
                        ln_lo_vector(dve, b + 1, 1 - par)
                    if proj and u - 1 in PROJ_AT:
                        proj_vector(dve, b + 1, 1 - par, PROJ_AT[u - 1])

            for item in range(A_ITEMS - 1):
                proj_vector(dve, 0, 0, item)
            with_pairs(dve, batch)
            turned_vector(dve, SEQS - 1, UPS - 1)
            for v in range(GU):
                finish(SEQS - 1, 1, v)

        def attn_scalar(act):
            def finish(b, v):
                if v == 5:
                    y_copy_scalar(act, b, G - 1)
                if v == 10:
                    y_copy2_scalar(act, b, G - 1)

            def batch(b, par, nxt, proj):
                for u in range(UPS):
                    exp_scalar(act, b, par, u)
                    if u % 2 == 0 and u >= 2:
                        turned_scalar(act, b, u - 2)
                    elif u == 0 and has_before(b):
                        turned_scalar(act, b - 1, UPS - 2)
                    g, v = divmod(u, GU)
                    if g == 0 and has_before(b):
                        finish(b - 1, v)
                    if g and v == 5:
                        y_copy_scalar(act, b, g - 1)
                    if g and v == 10:
                        y_copy2_scalar(act, b, g - 1)
                    if u == PROJ_LAST + 1:
                        proj_scalar(act, b, par, A_ITEMS - 1)
                    if u == LN_AT["hi"]:
                        ln_hi_scalar(act, b + 1, 1 - par)
                    if proj and u - 1 in PROJ_AT:
                        proj_scalar(act, b + 1, 1 - par, PROJ_AT[u - 1])

            for item in range(A_ITEMS - 1):
                proj_scalar(act, 0, 0, item)
            with_pairs(act, batch)
            turned_scalar(act, SEQS - 1, UPS - 2)
            for v in range(GU):
                finish(SEQS - 1, v)

        def attn_gpsimd(pool):
            def batch(b, par, nxt, proj):
                ln_rstd_gpsimd(pool, b + 1)
            with_pairs(pool, batch)

        def attn_sync(sp):
            def batch(b, par, nxt, proj):
                proj_sync(sp, b, G - 1, first=not has_before(b))
                if proj:
                    for g in range(G - 1):
                        proj_sync(sp, b + 1, g)
            for g in range(G - 1):
                proj_sync(sp, 0, g, first=True)
            with_pairs(sp, batch)

        def with_pairs(eng, batch):
            batch(0, 0, 1, True)
            batch(1, 1, 2, True)
            with eng.Fori(1, PAIRS - 1) as i:
                batch(2 * i, 0, 2 * i + 1, True)
                batch(2 * i + 1, 1, 2 * i + 2, True)
            batch(SEQS - 2, 0, SEQS - 1, True)
            batch(SEQS - 1, 1, 0, False)

        R_STEPS = 12

        def route_tensor(pe, f, b, par, n):
            z = fs[f]
            pe.wait_ge(s["ln_lo"], n + 1)
            if not (isinstance(b, int) and b == 0):
                pe.wait_ge(z["r_step"], (b - 1) * R_STEPS + 2)
            for t in range(QT):
                c = slice(t * P, (t + 1) * P)
                last = mm3(pe, ln_bank[:, t * E:(t + 1) * E], xh[par][:, c], xl[par][:, c], wr_h[:, :], wr_l[:, :])
            last.then_inc(z["log_mm"], 1)

        def route_a_vector(dve, f, b):
            z = fs[f]
            logits = ln_bank[:, 0:QT * E].rearrange("p (t e) -> p t e", t=QT)
            n = b * R_STEPS
            dve.wait_ge(z["log_mm"], b + 1)
            dve.tensor_reduce(r_max[:, :], logits, AX.X, ALU.max).then_inc(z["r_step"], 1)
            dve.wait_ge(z["r_step"], n + 1)
            dve.tensor_tensor(r_log[:, :, :], logits,
                              r_max[:, :].rearrange("p (t o) -> p t o", o=1).to_broadcast([P, QT, E]),
                              ALU.subtract).then_inc(z["r_step"], 1)

        def route_scalar(act, f, b):
            z = fs[f]
            act.wait_ge(z["r_step"], b * R_STEPS + 2)
            act.activation(r_exp[:, :, :], r_log[:, :, :], ACT.Exp).then_inc(z["r_exped"], 1)

        def route_b_vector(dve, f, b):
            z = fs[f]
            n = b * R_STEPS
            dve.wait_ge(z["r_exped"], b + 1)
            dve.tensor_reduce(r_sum[:, :], r_exp[:, :, :], AX.X, ALU.add).then_inc(z["r_step"], 1)
            dve.wait_ge(z["r_step"], n + 3)
            dve.reciprocal(r_one[:, :], r_sum[:, :]).then_inc(z["r_step"], 1)
            dve.wait_ge(z["r_step"], n + 4)
            dve.tensor_tensor(score[:, :, :], r_exp[:, :, :],
                              r_one[:, :].rearrange("p (t o) -> p t o", o=1).to_broadcast([P, QT, E]),
                              ALU.mult).then_inc(z["r_step"], 1)
            dve.wait_ge(z["r_step"], n + 5)
            for t in range(QT):
                other = score[:, t, :].rearrange("p (o j) -> p o j", o=1).to_broadcast([P, E, E])
                own = score[:, t, :].rearrange("p (e o) -> p e o", o=1).to_broadcast([P, E, E])
                dve.tensor_tensor(above[:, t, :, :], other, own, ALU.is_gt)
                last = dve.tensor_tensor(equal[:, t, :, :], other, own, ALU.is_equal)
            last.then_inc(z["r_step"], 1)

        def route_c_vector(dve, f, b):
            z = fs[f]
            n = b * R_STEPS
            dve.wait_ge(z["r_step"], n + 6)
            for t in range(QT):
                last = dve.tensor_tensor(equal[:, t, :, :], equal[:, t, :, :], tie[:, :, :], ALU.mult)
            last.then_inc(z["r_step"], 1)
            dve.wait_ge(z["r_step"], n + 7)
            dve.tensor_tensor(above[:, :, :, :].rearrange("p t e j -> p (t e j)"),
                              above[:, :, :, :].rearrange("p t e j -> p (t e j)"),
                              equal[:, :, :, :].rearrange("p t e j -> p (t e j)"), ALU.add).then_inc(z["r_step"], 1)
            dve.wait_ge(z["r_step"], n + 8)
            dve.tensor_reduce(rank[:, :, :], above[:, :, :, :], AX.X, ALU.add).then_inc(z["r_step"], 1)

        def route_d_vector(dve, f, b, par):
            z = fs[f]
            n = b * R_STEPS
            dve.wait_ge(z["r_step"], n + 9)
            dve.scalar_tensor_tensor(out=score[:, :, :], in0=rank[:, :, :], scalar=TOPK - 0.5, in1=score[:, :, :],
                                     op0=ALU.is_lt, op1=ALU.mult).then_inc(z["r_step"], 1)
            dve.wait_ge(z["r_step"], n + 10)
            dve.tensor_reduce(r_sum[:, :], score[:, :, :], AX.X, ALU.add).then_inc(z["r_step"], 1)
            dve.wait_ge(z["r_step"], n + 11)
            dve.tensor_scalar(r_max[:, :], r_sum[:, :], ROUTE_EPS, None, ALU.add).then_inc(z["r_step"], 1)
            dve.wait_ge(z["r_step"], n + 12)
            dve.reciprocal(r_one[:, :], r_max[:, :]).then_inc(z["log_read"], 1)
            dve.wait_ge(z["log_read"], b + 1)
            dve.tensor_tensor(gate[:, par, :, :], score[:, :, :],
                              r_one[:, :].rearrange("p (t o) -> p t o", o=1).to_broadcast([P, QT, E]),
                              ALU.mult).then_inc(z["gated"], 1)

        for f in range(2):
            fs[f]["log_read"] = sem(f"log_read_{f}")
            fs[f]["gated"] = sem(f"gated_{f}")
            fs[f]["y_ev"] = sem(f"y_exp_ev_{f}")
            fs[f]["y_back"] = sem(f"y_exp_back_{f}")

        def hidden_tensor(pe, f, b, par, k):
            z, m = fs[f], b * MU + k
            e, c = divmod(k, FC)
            cols = slice(c * P, (c + 1) * P)
            static_first = isinstance(b, int) and b == 0 and k < 2
            if not static_first:
                pe.wait_ge(z["silu_done"], m - 1)
            mm3(pe, bank[k % 2][:, :], wg_h[:, e, cols], wg_l[:, e, cols], xh[par][:, :],
                xl[par][:, :]).then_inc(z["gate_mm"], 1)
            if not static_first:
                pe.wait_ge(z["hid_done"], m - 1)
            last = mm3(pe, bank[2 + k % 2][:, :], wu_h[:, e, cols], wu_l[:, e, cols], xh[par][:, :], xl[par][:, :])
            last.then_inc(z["up_mm"], 1)

        def down_tensor(pe, f, b, par, k):
            z, m = fs[f], b * MU + k
            e, c = divmod(k, FC)
            o = bank[4 + (par * XP + e) % 2]
            if c == 0 and not (isinstance(b, int) and b == 0 and e < 2):
                pe.wait_ge(z["y_ev"], b * XP + e - 1)
            pe.wait_ge(z["hid_lo"], m + 1)
            h, l = hid_h[k % SLOTS][:, :], hid_l[k % SLOTS][:, :]
            w_h, w_l = wd_h[:, e, c, :], wd_l[:, e, c, :]
            mm = pe.matmul(o[:, :], w_h, h, start=(c == 0), stop=False)
            if k == MU - 1:
                mm.then_inc(s["xt_free"], 1)
            pe.matmul(o[:, :], w_l, h, start=False, stop=False)
            pe.matmul(o[:, :], w_h, l, start=False, stop=(c == FC - 1)).then_inc(z["down_used"], 1)

        def y_copy_expert(act, f, b, par, e):
            z, m = fs[f], b * XP + e
            act.wait_ge(z["down_used"], b * MU + (e + 1) * FC)
            if not (isinstance(b, int) and b == 0 and e < 2):
                act.wait_ge(z["y_back"], m - 1)
            act.activation(y_exp[:, (par * XP + e) % 2, :], bank[4 + (par * XP + e) % 2][:, :],
                           ACT.Copy).then_inc(z["y_ev"], 1)

        def y_back_expert(pe, f, b, par, e):
            z, m = fs[f], b * XP + e
            pe.wait_ge(z["y_ev"], m + 1)
            if not (isinstance(b, int) and b == 0 and e == 0):
                pe.wait_ge(z["acc_done"], m)
            for t in range(QT):
                cols = slice(t * P, (t + 1) * P)
                last = pe.transpose(bank[6][:, cols], y_exp[:, (par * XP + e) % 2, cols], ident[:, :])
            last.then_inc(z["y_back"], 1)

        def silu_scalar(act, f, b, k):
            z, m = fs[f], b * MU + k
            act.wait_ge(z["gate_mm"], m + 1)
            if not (isinstance(b, int) and b == 0 and k < 2):
                act.wait_ge(z["hid_done"], m - 1)
            act.activation(silu_g[:, k % 2, :], bank[k % 2][:, :], ACT.Silu).then_inc(z["silu_done"], 1)

        def hid_vector(dve, f, b, k):
            z, m = fs[f], b * MU + k
            dve.wait_ge(z["silu_done"], m + 1)
            dve.wait_ge(z["up_mm"], m + 1)
            if not (isinstance(b, int) and b == 0 and k < SLOTS):
                dve.wait_ge(z["hid_lo"], m - SLOTS + 1)
            dve.tensor_tensor(hid[:, k % SLOTS, :], bank[2 + k % 2][:, :], silu_g[:, k % 2, :],
                              ALU.mult).then_inc(z["hid_done"], 1)

        def hid_hi_scalar(act, f, b, k):
            z, m = fs[f], b * MU + k
            act.wait_ge(z["hid_done"], m + 1)
            if not (isinstance(b, int) and b == 0 and k < SLOTS):
                act.wait_ge(z["down_used"], m - SLOTS + 1)
            act.activation(hid_h[k % SLOTS][:, :], hid[:, k % SLOTS, :], ACT.Copy).then_inc(z["hid_hi"], 1)

        def hid_lo_gpsimd(pool, f, b, k):
            z, m = fs[f], b * MU + k
            pool.wait_ge(z["hid_hi"], m + 1)
            pool.tensor_tensor(hid_l[k % SLOTS][:, :], hid[:, k % SLOTS, :], hid_h[k % SLOTS][:, :],
                               ALU.subtract).then_inc(z["hid_lo"], 1)

        def add_vector(dve, f, b, par, e):
            z = fs[f]
            o = bank[6]
            dve.wait_ge(z["y_back"], b * XP + e + 1)
            if e == 0:
                xv = x_sb[:, bass.ds(b * QT, QT), :]
                dve.tensor_tensor(xv, o[:, :].rearrange("p (t d) -> p t d", t=QT), xv,
                                  ALU.add).then_inc(z["acc_done"], 1)
                return
            if e == 1:
                dve.wait_ge(z["gated"], b + 1)
            dve.wait_ge(z["acc_done"], b * XP + e)
            for t in range(QT):
                xt = x_sb[:, bass.ds(b * QT + t, 1), :].rearrange("p o d -> p (o d)")
                last = dve.scalar_tensor_tensor(out=xt, in0=o[:, t * P:(t + 1) * P], scalar=gate[:, par, t, e - 1:e],
                                                in1=xt, op0=ALU.mult, op1=ALU.add)
            last.then_inc(z["acc_done"], 1)

        LAG = SLOTS
        BACK_LAG = LAG + FC + 1
        F_LN = {"stats": 2, "norm": 4, "turn": 6, "hi": 7, "lo": 8, "route": 9, "route_a": 10, "route_b": 12,
                "route_c": 13, "route_d": 14}

        def ffn_tensor(pe, f, ph):
            def back(b, par, k):
                if k % FC == (BACK_LAG - 1) % FC:
                    e = (k - BACK_LAG) // FC
                    if e >= 0:
                        y_back_expert(pe, f, b, par, e)
                    elif has_before(b):
                        y_back_expert(pe, f, b - 1, 1 - par, XP + e)

            def batch(b, par, nxt, more):
                n = ph * SEQS + b
                for k in range(MU):
                    hidden_tensor(pe, f, b, par, k)
                    back(b, par, k)
                    if k >= LAG:
                        down_tensor(pe, f, b, par, k - LAG)
                    elif has_before(b):
                        down_tensor(pe, f, b - 1, 1 - par, MU + k - LAG)
                    if k == F_LN["turn"] and (more or ph < LAST):
                        ln_turn_tensor(pe, n + 1)
                    if k == F_LN["route"] and more:
                        route_tensor(pe, f, b + 1, 1 - par, n + 1)
            if ph:
                pe.wait_ge(s["x_done"], ph * SEQS)
            route_tensor(pe, f, 0, 0, ph * SEQS)
            with_pairs(pe, batch)
            for k in range(BACK_LAG + 1):
                if k < LAG:
                    down_tensor(pe, f, SEQS - 1, 1, MU + k - LAG)
                if k % FC == (BACK_LAG - 1) % FC and k < BACK_LAG:
                    y_back_expert(pe, f, SEQS - 1, 1, XP + (k - BACK_LAG) // FC)

        def ffn_vector(dve, f, ph):
            def finish(b, par, e):
                add_vector(dve, f, b, par, e)
                if e == XP - 1:
                    dve.wait_ge(fs[f]["acc_done"], b * XP + XP)
                    dve.sem_inc(s["x_done"], 1)

            def batch(b, par, nxt, more):
                n = ph * SEQS + b
                for k in range(MU):
                    hid_vector(dve, f, b, k)
                    e = (k - BACK_LAG - 1) // FC
                    if k % FC == BACK_LAG % FC:
                        if e >= 0:
                            finish(b, par, e)
                        elif has_before(b):
                            finish(b - 1, 1 - par, XP + e)
                    if more or ph < LAST:
                        if k == F_LN["stats"]:
                            ln_stats_vector(dve, n + 1, nxt)
                        if k == F_LN["norm"]:
                            ln_norm_vector(dve, n + 1, nxt)
                        if k == F_LN["lo"]:
                            ln_lo_vector(dve, n + 1, 1 - par)
                    if more and k == F_LN["route_a"]:
                        route_a_vector(dve, f, b + 1)
                    if more and k == F_LN["route_b"]:
                        route_b_vector(dve, f, b + 1)
                    if more and k == F_LN["route_c"]:
                        route_c_vector(dve, f, b + 1)
                    if more and k == F_LN["route_d"]:
                        route_d_vector(dve, f, b + 1, 1 - par)
            if ph:
                dve.wait_ge(s["x_done"], ph * SEQS)
            route_a_vector(dve, f, 0)
            route_b_vector(dve, f, 0)
            route_c_vector(dve, f, 0)
            route_d_vector(dve, f, 0, 0)
            with_pairs(dve, batch)
            for e in range((MU - 1 - BACK_LAG) // FC, XP):
                finish(SEQS - 1, 1, e)

        def ffn_scalar(act, f, ph):
            def batch(b, par, nxt, more):
                n = ph * SEQS + b
                for k in range(MU):
                    if k:
                        hid_hi_scalar(act, f, b, k - 1)
                    elif has_before(b):
                        hid_hi_scalar(act, f, b - 1, MU - 1)
                    silu_scalar(act, f, b, k)
                    if k % FC == LAG % FC:
                        e = (k - LAG - FC) // FC
                        if e >= 0:
                            y_copy_expert(act, f, b, par, e)
                        elif has_before(b):
                            y_copy_expert(act, f, b - 1, 1 - par, XP + e)
                    if k == F_LN["hi"] and (more or ph < LAST):
                        ln_hi_scalar(act, n + 1, 1 - par)
                    if more and k == F_LN["route_a"]:
                        route_scalar(act, f, b + 1)
            route_scalar(act, f, 0)
            with_pairs(act, batch)
            hid_hi_scalar(act, f, SEQS - 1, MU - 1)
            for e in range((MU - 1 - LAG) // FC, XP):
                y_copy_expert(act, f, SEQS - 1, 1, e)

        def ffn_gpsimd(pool, f, ph):
            def batch(b, par, nxt, more):
                n = ph * SEQS + b
                for k in range(MU):
                    hid_lo_gpsimd(pool, f, b, k)
                    if k == F_LN["stats"] - 1 and (more or ph < LAST):
                        ln_rstd_gpsimd(pool, n + 1)
            with_pairs(pool, batch)

        def flat_t(t):
            return t[:, :, :].rearrange("p t h -> p (t h)")

        def ssm_tensor(pe, ph):
            def in_proj(b, par):
                if has_before(b):
                    pe.wait_ge(s["yo_mul"], b * 2)
                    pe.wait_ge(s["y_sum"], b * 2)
                for q in range(XB):
                    c = slice(q * P, (q + 1) * P)
                    mm3(pe, bank[q][:, :], wx_h[:, c], wx_l[:, c], xh[par][:, :],
                        xl[par][:, :]).then_inc(s["xbc_mm"], 1)

            def add_states(b, ch):
                t, c = divmod(ch, CT)
                rows = slice(c * CH, (c + 1) * CH)
                if ch >= 2:
                    pe.wait_ge(s["st_add"], b * (NC - 1) + ch - 1)
                pe.matmul(bank[4 + ch % 2][:, 0:DI], b_tok[rows, t, :], x_dec[rows, t, :], start=True,
                          stop=True).then_inc(s["st_mm"], 1)

            def in_chunks(b, t):
                pe.wait_ge(s["mix_done"], b * 4 + t + 1)
                for g in range(SG):
                    for c in range(CT):
                        o = bank[2 + t // 2][c * CH:(c + 1) * CH, (t % 2) * DI + g * CH:(t % 2) * DI + (g + 1) * CH]
                        last = pe.matmul(o, decay[:, t, c, g, :], x_diag[:, t, c, g, :], start=True, stop=True)
                return last

            def batch(b, par, nxt, more):
                static0 = isinstance(b, int) and b == 0
                n = ph * SEQS + b
                for t in range(QT):
                    c = slice(t * P, (t + 1) * P)
                    if t >= 2:
                        pe.wait_ge(s["dt_read"], b * QT + t - 1)
                    elif not static0:
                        pe.wait_ge(s["yt_done"], b * 2)
                    mm3(pe, bank[4 + t % 2][:, 0:DI + NH], xh[par][:, c], xl[par][:, c], wz_h[:, :],
                        wz_l[:, :]).then_inc(s["zdt_mm"], 1)
                pe.wait_ge(s["act_x"], b * XB + XB)
                for t in range(QT):
                    for q in range(DI // P):
                        last = pe.transpose(bank[t // 2][:, (t % 2) * DI + q * P:(t % 2) * DI + (q + 1) * P],
                                            x_t[:, q, t * P:(t + 1) * P], ident[:, :])
                    if t == 0:
                        last.then_inc(s["xt_free"], 1)
                last.then_inc(s["xturn_mm"], 1)
                for t in range(QT):
                    last = pe.transpose(bank[2][:, t * P:(t + 1) * P], x_t[:, 2, t * P:(t + 1) * P], ident[:, :])
                last.then_inc(s["bturn_mm"], 1)
                for ch in range(NC):
                    c = slice(ch * CH, (ch + 1) * CH)
                    for r in range(CT):
                        last = pe.matmul(bank[3][r * CH:(r + 1) * CH, c], x_t[:, 2, c], x_t[:, 3, c], start=True, stop=True)
                last.then_inc(s["cb_mm"], 1)
                pe.wait_ge(s["a_done"], b + 1)
                pe.wait_ge(s["z_done"], b * QT + QT)
                pe.matmul(bank[4][:, 0:QT * NH], later[:, :], flat_t(a_tok), start=True, stop=True)
                pe.matmul(bank[4][:, QT * NH:2 * QT * NH], until[:, :], flat_t(a_tok), start=True, stop=True)
                for c in range(CT):
                    last = pe.matmul(bank[5][:, c * QT * NH:(c + 1) * QT * NH], in_chunk[:, c, :], flat_t(a_tok),
                                     start=True, stop=True)
                last.then_inc(s["dec_mm"], 1)
                pe.wait_ge(s["cum_done"], b + 1)
                pe.wait_ge(s["xdt_done"], b + 1)
                cum = a_cum[:, :, :].rearrange("p g l -> p (g l)")
                for i in range(NC * SG * CH // 512):
                    if i >= 2:
                        pe.wait_ge(s["diff_exp"], b * 8 + i - 1)
                    pe.matmul(bank[i % 2][:, :], later[:, :], cum[:, i * 512:(i + 1) * 512], start=True,
                              stop=True).then_inc(s["diff_mm"], 1)
                    if i == 2:
                        pe.wait_ge(s["xd_act"], b + 1)
                        pe.wait_ge(s["xd_dve"], b + 1)
                        pe.wait_ge(s["b_done"], b + 1)
                    if i >= 3 and i % 2:
                        in_chunks(b, (i - 3) // 2)
                pe.wait_ge(s["xdec_done"], b + 1)
                pe.wait_ge(s["dec_done"], b * 3 + 3)
                add_states(b, 0)
                add_states(b, 1)
                in_chunks(b, QT - 1).then_inc(s["yd_mm"], 1)
                for ch in range(2, NC - 1):
                    add_states(b, ch)
                if more or ph < LAST:
                    ln_turn_tensor(pe, n + 1)
                pe.wait_ge(s["diff_exp"], b * 8 + 8)
                for ch in range(NC):
                    t, c = divmod(ch, CT)
                    pe.wait_ge(s["st_add"], b * (NC - 1) + max(ch, 1))
                    last = pe.matmul(bank[t // 2][c * CH:(c + 1) * CH, (t % 2) * DI:(t % 2 + 1) * DI],
                                     x_t[:, 3, ch * CH:(ch + 1) * CH], state[:, ch, :], start=True, stop=True)
                last.then_inc(s["yo_mm"], 1)
                if more:
                    in_proj(b + 1, 1 - par)
                pe.wait_ge(s["y_zmul"], b + 1)
                for q in range(DI // P):
                    for t in range(QT):
                        last = pe.transpose(bank[4 + q][:, t * P:(t + 1) * P], y[:, t, q * P:(q + 1) * P], ident[:, :])
                last.then_inc(s["yt_mm"], 1)
                pe.wait_ge(s["yt_done"], b * 2 + 2)
                if not static0:
                    pe.wait_ge(s["x_done"], n)
                for t in range(QT):
                    for q in range(DI // P):
                        last = pe.matmul(bank[6][:, t * D:(t + 1) * D], y_ch[:, q, t * P:(t + 1) * P], w_out[:, q, :],
                                         start=(q == 0), stop=(q == DI // P - 1))
                last.then_inc(s["so_mm"], 1)
            pe.wait_ge(s["m_split"], 1)
            pe.wait_ge(s["m_const"], 1)
            in_proj(0, 0)
            with_pairs(pe, batch)

        def ssm_vector(dve, ph):
            dve.wait_ge(s["x_done"], ph * SEQS)
            dve.wait_ge(s["m_hi"], 1)
            dve.tensor_tensor(wx_l[:, :], wx_st[:, :], wx_h[:, :], ALU.subtract)
            dve.tensor_tensor(wz_l[:, :], wz_st[:, :], wz_h[:, :], ALU.subtract).then_inc(s["m_split"], 1)
            dve.tensor_scalar(neg_a[:, :], neg_a[:, :], -1.0, None, ALU.mult).then_inc(s["m_nega"], 1)
            dve.memset(x_diag[:, :, :, :, :].rearrange("p t c g x -> p (t c g x)"), 0.0).then_inc(s["m_zeroed"], 1)
            dve.wait_ge(s["m_zeroed"], 1)
            dve.wait_ge(s["m_nega"], 1)
            dve.wait_ge(s["m_const"], 1)

            def conv(b):
                for q in range(XB):
                    dve.wait_ge(s["xbc_mm"], b * XB + q + 1)
                    if q == 0 and has_before(b):
                        dve.wait_ge(s["yo_mm"], b)
                    dve.tensor_scalar(x_t[:, q, :], bank[q][:, :], conv_w[:, q, TAPS - 1:TAPS], conv_b[:, q:q + 1],
                                      ALU.mult, ALU.add).then_inc(s["conv_step"], 1)
                    for k in range(1, TAPS):
                        dve.wait_ge(s["conv_step"], (b * XB + q) * TAPS + k)
                        dve.scalar_tensor_tensor(out=x_t[:, q, k:L], in0=bank[q][:, 0:L - k],
                                                 scalar=conv_w[:, q, TAPS - 1 - k:TAPS - k], in1=x_t[:, q, k:L],
                                                 op0=ALU.mult, op1=ALU.add).then_inc(s["conv_step"], 1)

            def batch(b, par, nxt, more):
                static0 = isinstance(b, int) and b == 0
                n = ph * SEQS + b
                for t in range(QT):
                    dve.wait_ge(s["z_done"], b * QT + t + 1)
                    dve.tensor_tensor(dt_v[:, t, :], bank[4 + t % 2][:, DI:DI + NH], dt_bias[:, :],
                                      ALU.add).then_inc(s["dt_read"], 1)
                dve.wait_ge(s["dt_read"], b * QT + QT)
                steps = b * DT_STEPS

                def step(r):
                    dve.wait_ge(s["dt_step"], steps + r)

                dve.tensor_scalar(dt_r[:, :, :], dt_v[:, :, :], 0.0, None, ALU.max).then_inc(s["dt_step"], 1)
                step(1)
                dve.scalar_tensor_tensor(out=dt_s[:, :, :], in0=dt_r[:, :, :], scalar=2.0, in1=dt_v[:, :, :],
                                         op0=ALU.mult, op1=ALU.subtract).then_inc(s["dt_step"], 1)
                dve.wait_ge(s["dt_exp"], b + 1)
                dve.tensor_scalar(dt_q[:, :, :], dt_e[:, :, :], 2.0, None, ALU.add).then_inc(s["dt_step"], 1)
                step(3)
                dve.reciprocal(dt_p[:, :, :], dt_q[:, :, :]).then_inc(s["dt_step"], 1)
                step(4)
                dve.tensor_tensor(dt_q[:, :, :], dt_e[:, :, :], dt_p[:, :, :], ALU.mult).then_inc(s["dt_step"], 1)
                step(5)
                dve.tensor_tensor(dt_s[:, :, :], dt_q[:, :, :], dt_q[:, :, :], ALU.mult).then_inc(s["dt_step"], 1)
                step(6)
                dve.tensor_scalar(dt_p[:, :, :], dt_s[:, :, :], ATANH[0], None, ALU.mult).then_inc(s["dt_step"], 1)
                r = 7
                for coefficient in ATANH[1:]:
                    step(r)
                    dve.scalar_tensor_tensor(out=dt_p[:, :, :], in0=dt_p[:, :, :], scalar=coefficient, in1=dt_s[:, :, :],
                                             op0=ALU.add, op1=ALU.mult).then_inc(s["dt_step"], 1)
                    r += 1
                step(r)
                dve.scalar_tensor_tensor(out=dt_p[:, :, :], in0=dt_p[:, :, :], scalar=1.0, in1=dt_q[:, :, :], op0=ALU.add,
                                         op1=ALU.mult).then_inc(s["dt_step"], 1)
                step(r + 1)
                dve.scalar_tensor_tensor(out=dt[:, :, :], in0=dt_p[:, :, :], scalar=2.0, in1=dt_r[:, :, :], op0=ALU.mult,
                                         op1=ALU.add).then_inc(s["dt_step"], 1)
                step(r + 2)
                assert r + 2 == DT_STEPS
                dve.tensor_tensor(a_tok[:, :, :], dt[:, :, :],
                                  neg_a[:, :].rearrange("p (o h) -> p o h", o=1).to_broadcast([P, QT, NH]),
                                  ALU.mult).then_inc(s["a_done"], 1)
                dve.wait_ge(s["a_done"], b + 1)
                for c in range(CT):
                    for j in range(CT):
                        last = dve.tensor_copy(a_row[j * CH:(j + 1) * CH, :, c, :],
                                               a_tok[c * CH:(c + 1) * CH, :, :].rearrange("p t (g j) -> p t g j",
                                                                                         j=CT)[:, :, :, j])
                last.then_inc(s["a_rows"], 1)
                dve.wait_ge(s["a_rows"], b + 1)
                if not static0:
                    dve.wait_ge(s["yo_mm"], b)
                dve.tensor_tensor(a_cum[:, :, :],
                                  a_row[:, :, :, :].rearrange("p t c (g o) -> p (t c g) o", o=1)
                                  .to_broadcast([P, NC * SG, CH]),
                                  until_row[:, :].rearrange("p (o l) -> p o l", o=1).to_broadcast([P, NC * SG, CH]),
                                  ALU.mult).then_inc(s["cum_done"], 1)
                dve.wait_ge(s["xturn_mm"], b + 1)
                for i in range(QT // 2):
                    last = dve.tensor_tensor(
                        x_dt[:, 2 * i:2 * i + 2, :].rearrange("p t (h c) -> p (t h) c", c=HP),
                        bank[i][:, :].rearrange("p (h c) -> p h c", c=HP),
                        dt[:, 2 * i:2 * i + 2, :].rearrange("p t (h o) -> p (t h) o", o=1).to_broadcast([P, 2 * NH, HP]),
                        ALU.mult)
                last.then_inc(s["xdt_done"], 1)
                dve.wait_ge(s["xdt_done"], b + 1)
                for c in range(CT // 2, CT):
                    for j in range(CT):
                        last = dve.tensor_copy(
                            x_diag[j * CH:(j + 1) * CH, :, c, :, j * HP:(j + 1) * HP],
                            x_dt[c * CH:(c + 1) * CH, :, :].rearrange("p t (g j x) -> p t g j x", g=SG, j=CT)[:, :, :, j, :])
                last.then_inc(s["xd_dve"], 1)
                dve.wait_ge(s["cb_mm"], b + 1)
                dve.tensor_tensor(cb[:, :, :], bank[3][:, :].rearrange("p (c l) -> p c l", c=NC),
                                  until_row[:, :].rearrange("p (o l) -> p o l", o=1).to_broadcast([P, NC, CH]),
                                  ALU.mult).then_inc(s["cb_done"], 1)
                dve.wait_ge(s["dec_done"], b * 3 + 1)
                dve.tensor_tensor(x_dec[:, :, :].rearrange("p t (h c) -> p (t h) c", c=HP),
                                  x_dt[:, :, :].rearrange("p t (h c) -> p (t h) c", c=HP),
                                  e_end[:, :, :].rearrange("p t (h o) -> p (t h) o", o=1).to_broadcast([P, QT * NH, HP]),
                                  ALU.mult).then_inc(s["xdec_done"], 1)
                if more or ph < LAST:
                    ln_stats_vector(dve, n + 1, nxt)
                dve.wait_ge(s["cb_done"], b + 1)
                for t in range(QT):
                    dve.wait_ge(s["diff_exp"], b * 8 + 2 * t + 2)
                    for c in range(CT):
                        last = dve.tensor_tensor(decay[:, t, c, :, :], decay[:, t, c, :, :],
                                                 cb[:, t * CT + c:t * CT + c + 1, :].to_broadcast([P, SG, CH]), ALU.mult)
                    last.then_inc(s["mix_done"], 1)
                if more or ph < LAST:
                    ln_norm_vector(dve, n + 1, nxt)
                for ch in range(NC - 1):
                    t, c = divmod(ch, CT)
                    k = b * (NC - 1) + ch
                    if ch:
                        dve.wait_ge(s["st_add"], k)
                        if ch == 1:
                            dve.wait_ge(s["dec_done"], b * 3 + 3)
                        dve.tensor_tensor(s_dec[:, :].rearrange("p (h c) -> p h c", c=HP),
                                          state[:, ch, :].rearrange("p (h c) -> p h c", c=HP),
                                          e_tot[:, c, t, :].rearrange("p (h o) -> p h o", o=1).to_broadcast([P, NH, HP]),
                                          ALU.mult).then_inc(s["st_mul"], 1)
                        dve.wait_ge(s["st_mul"], b * (NC - 2) + ch)
                        dve.wait_ge(s["st_mm"], k + 1)
                        dve.tensor_tensor(state[:, ch + 1, :], bank[4 + ch % 2][:, 0:DI], s_dec[:, :],
                                          ALU.add).then_inc(s["st_add"], 1)
                    else:
                        dve.wait_ge(s["st_mm"], k + 1)
                        if not static0:
                            dve.wait_ge(s["yo_mm"], b)
                        dve.memset(state[:, 0, :], 0.0)
                        dve.tensor_copy(state[:, 1, :], bank[4][:, 0:DI]).then_inc(s["st_add"], 1)
                if more or ph < LAST:
                    ln_lo_vector(dve, n + 1, 1 - par)
                dve.wait_ge(s["yo_mm"], b + 1)
                if not static0:
                    dve.wait_ge(s["yt_mm"], b)
                for i in range(QT // 2):
                    dve.tensor_tensor(
                        y[:, 2 * i:2 * i + 2, :].rearrange("p t (h c) -> p (t h) c", c=HP),
                        bank[i][:, :].rearrange("p (h c) -> p h c", c=HP),
                        e_cum[:, 2 * i:2 * i + 2, :].rearrange("p t (h o) -> p (t h) o", o=1).to_broadcast([P, 2 * NH, HP]),
                        ALU.mult).then_inc(s["yo_mul"], 1)
                dve.wait_ge(s["yd_mm"], b + 1)
                for i in range(QT // 2):
                    dve.wait_ge(s["yo_mul"], b * 2 + i + 1)
                    dve.tensor_tensor(y[:, 2 * i:2 * i + 2, :].rearrange("p t x -> p (t x)"), bank[2 + i][:, :],
                                      y[:, 2 * i:2 * i + 2, :].rearrange("p t x -> p (t x)"),
                                      ALU.add).then_inc(s["y_sum"], 1)
                dve.wait_ge(s["y_sum"], b * 2 + 2)
                for t in range(QT):
                    dve.bn_stats(y_stats[:, t, :], y[:, t, :])
                dve.drain()
                for t in range(QT):
                    last = dve.bn_aggr(y_mv[:, t, :], y_stats[:, t, :])
                last.then_inc(s["y_mvd"], 1)
                dve.wait_ge(s["y_mvd"], b + 1)
                dve.tensor_scalar(y_var[:, :], y_mv[:, :, 1], LN_EPS, None, ALU.add).then_inc(s["y_eps"], 1)
                dve.wait_ge(s["y_pow"], b + 1)
                for t in range(QT):
                    last = dve.tensor_scalar(y[:, t, :], y[:, t, :], y_mv[:, t, 0:1], y_rstd[:, t:t + 1], ALU.subtract,
                                             ALU.mult)
                last.then_inc(s["y_nrm"], 1)
                dve.wait_ge(s["y_nrm"], b + 1)
                dve.tensor_tensor(y[:, :, :], y[:, :, :],
                                  y_w[:, :].rearrange("p (o x) -> p o x", o=1).to_broadcast([P, QT, DI]),
                                  ALU.mult).then_inc(s["y_wmul"], 1)
                dve.wait_ge(s["y_wmul"], b + 1)
                dve.tensor_tensor(y[:, :, :], y[:, :, :], z_s[:, :, :], ALU.mult).then_inc(s["y_zmul"], 1)
                if more:
                    conv(b + 1)
                dve.wait_ge(s["so_mm"], b + 1)
                xv = x_sb[:, bass.ds(b * QT, QT), :]
                dve.tensor_tensor(xv, bank[6][:, :].rearrange("p (t d) -> p t d", t=QT), xv,
                                  ALU.add).then_inc(s["x_done"], 1)
            conv(0)
            with_pairs(dve, batch)

        DT_STEPS = 7 + len(ATANH) - 1 + 2

        def ssm_scalar(act, ph):
            act.wait_ge(s["m_loaded"], 16 * N_M)
            act.activation(wx_h[:, :], wx_st[:, :], ACT.Copy)
            act.activation(neg_a[:, :], neg_a[:, :], ACT.Exp)
            act.activation(wz_h[:, :], wz_st[:, :], ACT.Copy).then_inc(s["m_hi"], 1)

            def batch(b, par, nxt, more):
                static0 = isinstance(b, int) and b == 0
                n = ph * SEQS + b
                for t in range(QT):
                    if t == 2:
                        for q in range(XB):
                            act.wait_ge(s["conv_step"], (b * XB + q + 1) * TAPS)
                            act.activation(x_t[:, q, :], x_t[:, q, :], ACT.Silu).then_inc(s["act_x"], 1)
                    act.wait_ge(s["zdt_mm"], b * QT + t + 1)
                    if t == 0 and not static0:
                        act.wait_ge(s["y_zmul"], b)
                    act.activation(z_s[:, t, :], bank[4 + t % 2][:, 0:DI], ACT.Silu).then_inc(s["z_done"], 1)
                act.wait_ge(s["dt_step"], b * DT_STEPS + 2)
                act.activation(dt_e[:, :, :], dt_s[:, :, :], ACT.Exp, scale=-1.0).then_inc(s["dt_exp"], 1)
                act.wait_ge(s["bturn_mm"], b + 1)
                act.activation(b_tok[:, :, :], bank[2][:, :].rearrange("p (t n) -> p t n", t=QT),
                               ACT.Copy).then_inc(s["b_done"], 1)
                act.wait_ge(s["dec_mm"], b + 1)
                act.activation(flat_t(e_end), bank[4][:, 0:QT * NH], ACT.Exp).then_inc(s["dec_done"], 1)
                act.activation(flat_t(e_cum), bank[4][:, QT * NH:2 * QT * NH], ACT.Exp).then_inc(s["dec_done"], 1)
                act.activation(e_tot[:, :, :, :].rearrange("p c t h -> p (c t h)"), bank[5][:, :],
                               ACT.Exp).then_inc(s["dec_done"], 1)
                act.wait_ge(s["xdt_done"], b + 1)
                for c in range(CT // 2):
                    for j in range(CT):
                        last = act.activation(
                            x_diag[j * CH:(j + 1) * CH, :, c, :, j * HP:(j + 1) * HP],
                            x_dt[c * CH:(c + 1) * CH, :, :].rearrange("p t (g j x) -> p t g j x", g=SG, j=CT)[:, :, :, j, :],
                            ACT.Copy)
                last.then_inc(s["xd_act"], 1)
                dec = decay[:, :, :, :, :].rearrange("p t c g l -> p (t c g l)")
                for i in range(8):
                    act.wait_ge(s["diff_mm"], b * 8 + i + 1)
                    act.activation(dec[:, i * 512:(i + 1) * 512], bank[i % 2][:, :], ACT.Exp).then_inc(s["diff_exp"], 1)
                if more or ph < LAST:
                    ln_hi_scalar(act, n + 1, 1 - par)
                for q in range(DI // P):
                    act.wait_ge(s["yt_mm"], b + 1)
                    act.activation(y_ch[:, q, :], bank[4 + q][:, :], ACT.Copy).then_inc(s["yt_done"], 1)
            act.wait_ge(s["m_zeroed"], 1)
            with_pairs(act, batch)

        def ssm_gpsimd(pool, ph):
            pool.wait_ge(s["x_done"], SEQS)
            pool.memset(blocks[:, :], 0.0)
            pool.memset(in_chunk[:, :, :], 0.0).then_inc(s["m_ones"], 1)
            pool.wait_ge(s["m_ones"], 1)
            for c in range(CT):
                rows = slice(c * CH, (c + 1) * CH)
                pool.memset(in_chunk[rows, c, :], 1.0)
                last = pool.memset(blocks[rows, rows], 1.0)
            last.then_inc(s["m_ones"], 1)
            pool.wait_ge(s["m_ones"], 2)
            pool.affine_select(out=later[:, :], in_=blocks[:, :], compare_op=ALU.is_gt, fill=0.0, base=0,
                               pattern=[[-1, P]], channel_multiplier=1)
            pool.affine_select(out=until[:, :], in_=blocks[:, :], compare_op=ALU.is_ge, fill=0.0, base=0,
                               pattern=[[1, P]], channel_multiplier=-1).then_inc(s["m_tri"], 1)
            pool.wait_ge(s["m_tri"], 1)
            for c in range(CT):
                rows = slice(c * CH, (c + 1) * CH)
                last = pool.tensor_copy(until_row[rows, :], until[rows, rows])
            last.then_inc(s["m_const"], 1)

            def batch(b, par, nxt, more):
                if more or ph < LAST:
                    ln_rstd_gpsimd(pool, ph * SEQS + b + 1)
                pool.wait_ge(s["y_eps"], b + 1)
                pool.tensor_tensor(y_rstd[:, :], y_var[:, :], half_neg[:, :], ALU.pow).then_inc(s["y_pow"], 1)
            with_pairs(pool, batch)

        N_M = 9

        def ssm_sync(sp, ph):
            if ph:
                sp.wait_ge(s["x_done"], SEQS)
            for dst, src in (
                (wx_st[:, :], w["in_wT"][:, DI:DI + XB * P]),
                (wz_st[:, 0:DI], w["in_wT"][:, 0:DI]),
                (wz_st[:, DI:DI + NH], w["in_wT"][:, DI + XB * P:DI + XB * P + NH]),
                (w_out[:, :, :], w["out_wT"].rearrange("(q p) d -> p q d", p=P)),
                (conv_w[:, :, :], w["conv_w"].rearrange("(q p) k -> p q k", p=P)),
                (conv_b[:, :], w["conv_b"]),
                (dt_bias[:, :], w["dt_bias"].rearrange("(o h) -> o h", o=1).to_broadcast([P, NH])),
                (neg_a[:, :], w["A_log"].rearrange("(o h) -> o h", o=1).to_broadcast([P, NH])),
                (y_w[:, :], w["ln_w"].rearrange("(o x) -> o x", o=1).to_broadcast([P, DI])),
            ):
                sp.dma_start(dst, src).then_inc(s["m_loaded"], 16)

        def flat3(t):
            return t[:, :, :].rearrange("p e f -> p (e f)")

        def flat4(t):
            return t[:, :, :, :].rearrange("p e c d -> p (e c d)")

        W_SPLITS = [[flat3(t) for t in (wg_st, wg_h, wg_l)], [flat3(t) for t in (wu_st, wu_h, wu_l)],
                    [flat4(t) for t in (wd_st, wd_h, wd_l)], [t[:, :] for t in (wr_st, wr_h, wr_l)]]

        @block.sync
        def _(sp):
            sp.dma_start(x_sb[:, 0:QT, :], x_in[0].rearrange("(t p) d -> p t d", p=P)).then_inc(s["x0_loaded"], 16)
            n_w = 0
            for dst, src in (
                (wqT_st[:, :, :], w["WqT"].rearrange("h k d -> k h d")),
                (wkT_st[:, :, :], w["WkT"].rearrange("h k c -> k h c")),
                (wkv_st[:, :], w["Wkv_down"]),
                (wvT_st[:, :, :], w["WvT"].rearrange("h k c -> k h c")),
                (wo_st[:, :, :], w["Wout"].rearrange("h k d -> k h d")),
                (wr_st[:, :], w["Wr"]),
                (wg_st[:, 0, :], w["Sg"]), (wg_st[:, 1:XP, :], w["Wg"].rearrange("e h f -> h e f")),
                (wu_st[:, 0, :], w["Su"]), (wu_st[:, 1:XP, :], w["Wu"].rearrange("e h f -> h e f")),
                (wd_st[:, 0, :, :], w["Sd"].rearrange("(c p) d -> p c d", p=P)),
                (wd_st[:, 1:XP, :, :].rearrange("p e c d -> p (e c) d"),
                 w["Wd"].rearrange("e (c p) d -> p (e c) d", p=P)),
            ):
                sp.dma_start(dst, src).then_inc(s["w_loaded"], 16)
                n_w += 1
            assert n_w == N_W
            for q in range(1, SEQS):
                sp.dma_start(x_sb[:, q * QT:(q + 1) * QT, :],
                             x_in[q].rearrange("(t p) d -> p t d", p=P)).then_inc(s["x_loaded"], 16)
            if "attn" in phases:
                attn_sync(sp)
            if "ssm" in phases:
                ssm_sync(sp, phases.index("ssm"))
            with sp.Fori(0, SEQS) as b:
                sp.wait_ge(s["x_done"], LAST * SEQS + 1 + b)
                sp.dma_start(out[bass.ds(b, 1), :, :].rearrange("o (t p) d -> p (o t) d", p=P),
                             x_sb[:, bass.ds(b * QT, QT), :]).then_inc(s["stored"], 16)
            sp.wait_ge(s["stored"], 16 * SEQS)

        @block.gpsimd
        def _(pool):
            pool.memset(ident[:, :], 0.0)
            pool.memset(causal[:, :], 0.0)
            pool.memset(tie[:, :, :], 1.0)
            pool.memset(half_neg[:, :], -0.5).then_inc(s["c_zero"], 1)
            pool.wait_ge(s["c_zero"], 1)
            pool.affine_select(out=ident[:, :], in_=ident[:, :], compare_op=ALU.not_equal, fill=1.0, base=0,
                               pattern=[[-1, P]], channel_multiplier=1)
            pool.affine_select(out=causal[:, :], in_=causal[:, :], compare_op=ALU.is_ge, fill=MASKED, base=0,
                               pattern=[[-1, P]], channel_multiplier=1)
            pool.affine_select(out=tie[:, :, :], in_=tie[:, :, :], compare_op=ALU.is_gt, fill=0.0, base=0,
                               pattern=[[1, E], [-1, E]], channel_multiplier=0).then_inc(s["c_made"], 1)
            ln_rstd_gpsimd(pool, 0)
            for ph, name in enumerate(phases):
                if name == "attn":
                    attn_gpsimd(pool)
                elif name == "ssm":
                    ssm_gpsimd(pool, ph)
                else:
                    ffn_gpsimd(pool, FN[ph], ph)

        @block.tensor
        def _(pe):
            pe.sem_inc(s["xt_free"], 1)
            pe.wait_ge(s["w_loaded"], 16 * N_W)
            for h in range(H):
                pe.matmul(bank[0][:, h * LD:(h + 1) * LD], wqT_st[:, h, :], wkT_st[:, h, :], start=True, stop=True)
            for h in range(H):
                g, j = divmod(h, HG)
                last = pe.matmul(bank[1][j * LD:(j + 1) * LD, g * D:(g + 1) * D], wvT_st[:, h, :], wo_st[:, h, :],
                                 start=True, stop=True)
            last.then_inc(s["wfold_mm"], 1)
            pe.wait_ge(s["c_made"], 1)
            ln_turn_tensor(pe, 0, first=True)
            pe.wait_ge(s["c_round"], 1)
            pe.wait_ge(s["wfold_done"], 1)
            for ph, name in enumerate(phases):
                if name == "attn":
                    attn_tensor(pe)
                elif name == "ssm":
                    ssm_tensor(pe, ph)
                else:
                    ffn_tensor(pe, FN[ph], ph)

        @block.scalar
        def _(act):
            act.wait_ge(s["w_loaded"], 16 * N_W)
            for st, hi, lo in W_SPLITS:
                act.activation(hi, st, ACT.Copy)
            for r in range(HG):
                last = act.activation(wkv_h[:, r, :], wkv_st[:, :], ACT.Copy)
            last.then_inc(s["w_hi"], 1)
            act.wait_ge(s["wfold_mm"], 1)
            act.activation(wq_h[:, :], bank[0][:, :], ACT.Copy, scale=HD ** -0.5).then_inc(s["wfold_hi"], 1)
            ln_hi_scalar(act, 0, 0, first=True)
            for ph, name in enumerate(phases):
                if name == "attn":
                    attn_scalar(act)
                elif name == "ssm":
                    ssm_scalar(act, ph)
                else:
                    ffn_scalar(act, FN[ph], ph)

        @block.vector
        def _(dve):
            dve.wait_ge(s["x0_loaded"], 16)
            ln_stats_vector(dve, 0, 0)
            dve.wait_ge(s["c_made"], 1)
            dve.tensor_copy(ident_r[:, :], ident[:, :])
            dve.tensor_copy(causal_r[:, :], causal[:, :]).then_inc(s["c_round"], 1)
            ln_norm_vector(dve, 0, 0, first=True)
            dve.wait_ge(s["w_hi"], 1)
            for st, hi, lo in W_SPLITS:
                dve.tensor_tensor(lo, st, hi, ALU.subtract)
            for r in range(HG):
                dve.tensor_tensor(wkv_l[:, r, :], wkv_st[:, :], wkv_h[:, r, :], ALU.subtract)
            dve.wait_ge(s["wfold_hi"], 1)
            dve.scalar_tensor_tensor(out=wq_l[:, :], in0=bank[0][:, :], scalar=HD ** -0.5, in1=wq_h[:, :],
                                     op0=ALU.mult, op1=ALU.subtract)
            dve.tensor_copy(wvo[:, :, :], bank[1][:, :].rearrange("p (g d) -> p g d", g=G)).then_inc(s["wfold_done"], 1)
            ln_lo_vector(dve, 0, 0)
            dve.wait_ge(s["x_loaded"], 16 * (SEQS - 1))
            for ph, name in enumerate(phases):
                if name == "attn":
                    attn_vector(dve)
                elif name == "ssm":
                    ssm_vector(dve, ph)
                else:
                    ffn_vector(dve, FN[ph], ph)


PHASES = ("attn", "ffn", "ssm", "ffn")


def kernel(**inputs):
    import numpy as np
    import concourse.bacc as bacc
    from concourse.bass_utils import run_bass_kernel_spmd as run

    a = {k: np.asarray(v) for k, v in inputs.items()}
    arrays = {
        "x": a["L0_attn_a_x_bld"],
        "WqT": a["L0_attn_a_Wq"].transpose(1, 2, 0),
        "Wkv_down": a["L0_attn_a_Wkv_down"],
        "WkT": a["L0_attn_a_Wk_up"].transpose(1, 2, 0),
        "WvT": a["L0_attn_a_Wv_up"].transpose(1, 2, 0),
        "Wout": a["L0_attn_a_Wout"],
        "Wr": a["L0_ffn_Wr"], "Wg": a["L0_ffn_Wg"], "Wu": a["L0_ffn_Wu"], "Wd": a["L0_ffn_Wd"],
        "in_wT": a["L0_attn_b_in_proj_w"].T, "out_wT": a["L0_attn_b_out_proj_w"].T,
        "conv_w": a["L0_attn_b_conv_w"], "conv_b": a["L0_attn_b_conv_b"].reshape(XB, P).T, "dt_bias": a["L0_attn_b_dt_bias"],
        "A_log": a["L0_attn_b_A_log"], "ln_w": a["L0_attn_b_ln_w"],
        "Sg": a["L0_ffn_Sg"], "Su": a["L0_ffn_Su"], "Sd": a["L0_ffn_Sd"],
    }
    arrays = {k: np.ascontiguousarray(v) for k, v in arrays.items()}
    nc = bacc.Bacc("TRN2", target_bir_lowering=False, num_devices=1)
    w = {k: nc.dram_tensor(f"in_{k}", v.shape, F32, kind="ExternalInput").ap() for k, v in arrays.items()}
    out = nc.dram_tensor("out", arrays["x"].shape, F32, kind="ExternalOutput").ap()
    program(nc, w["x"], out, w, PHASES)
    r = run(nc, [{f"in_{k}": v for k, v in arrays.items()}], core_ids=[0])
    return r.results[0]["out"]
```
